# Optimizing a Trainium2 kernel written in Bass

```python
import numpy as np
import jax
import jax.numpy as jnp

def _softmax(x, axis=-1):
    return jax.nn.softmax(x, axis=axis)

def _gelu(x):
    return jax.nn.gelu(x, approximate=True)

def _silu(x):
    return jax.nn.silu(x)

def _sigmoid(x):
    return jax.nn.sigmoid(x)

def _layernorm(x, axis=-1, eps=1e-05):
    m = jnp.mean(x, axis=axis, keepdims=True)
    v = jnp.var(x, axis=axis, keepdims=True)
    return (x - m) / jnp.sqrt(v + eps)

def _scatter_add(tgt, idx, src, axis=0):
    return tgt.at[idx].add(src)

def _segment_sum(src, seg, n):
    return jax.ops.segment_sum(src, seg, n)
kernel_name = 'mk_gps_d1_gnn_r32_007abe'

def setup_inputs(seed: int=0):
    np.random.seed(seed)
    _w = jnp.asarray

    def _rec_inputs():
        import jax
        import jax.numpy as jnp
        _gk = jax.random.key(seed)
        x = -0.0002117 + 1 * jax.random.normal(jax.random.fold_in(_gk, 1), (3125, 256), jnp.float32)
        _s = jax.random.randint(jax.random.fold_in(_gk, 2), (25000,), 0, 3125, jnp.int32)
        _d = jax.random.randint(jax.random.fold_in(_gk, 3), (25000,), 0, 3125, jnp.int32)
        _loop = jnp.arange(3125, dtype=jnp.int32)
        src = jnp.concatenate([_s, _d, _loop])
        dst = jnp.concatenate([_d, _s, _loop])
        _o = jnp.argsort(dst, stable=True)
        src = src[_o]
        dst = dst[_o]
        return (x, src, dst)
    x, src, dst = _rec_inputs()

    def _L0_gnn_setup():
        import jax, jax.numpy as jnp
        import numpy as np
        N_NODES = 3125
        N_EDGES = 100000
        D = 256
        key = jax.random.key(seed)
        ks = jax.random.split(key, 6)
        x = jax.random.normal(ks[0], (N_NODES, D), dtype=jnp.float32)
        edge_src = jax.random.randint(ks[1], (N_EDGES,), 0, N_NODES, dtype=jnp.int32)
        edge_dst = jax.random.randint(ks[2], (N_EDGES,), 0, N_NODES, dtype=jnp.int32)
        w = jnp.ones((1,), dtype=jnp.float32) * 3.0
        W1 = jax.random.normal(ks[3], (64, D), dtype=jnp.float32) * 0.05
        W2 = jax.random.normal(ks[4], (32, 64), dtype=jnp.float32) * 0.1
        W3 = jax.random.normal(ks[5], (D, 32), dtype=jnp.float32) * 0.1
        return {'x': x, 'edge_src': edge_src, 'edge_dst': edge_dst, 'w': w, 'W1': W1, 'W2': W2, 'W3': W3}
    _L0_gnn_all = _L0_gnn_setup()
    _L0_gnn_in = {k: v for k, v in _L0_gnn_all.items() if k in ('w', 'W1', 'W2', 'W3')}
    del _L0_gnn_all

    def _L0_mix_setup():
        import jax, jax.numpy as jnp
        import numpy as np
        NUM_HEADS = 8
        key = jax.random.key(seed)
        ks = jax.random.split(key, 5)
        B, N, C = (8, 512, 256)
        x = jax.random.normal(ks[0], (B, N, C), dtype=jnp.float32)
        Wq = jax.random.normal(ks[1], (C, C), dtype=jnp.float32) * 0.02
        Wkv = jax.random.normal(ks[2], (2 * C, C), dtype=jnp.float32) * 0.02
        Wproj = jax.random.normal(ks[3], (C, C), dtype=jnp.float32) * 0.02
        bproj = jnp.zeros((C,), dtype=jnp.float32)
        return {'x': x, 'Wq': Wq, 'Wkv': Wkv, 'Wproj': Wproj, 'bproj': bproj}
    _L0_mix_all = _L0_mix_setup()
    _L0_mix_in = {k: v for k, v in _L0_mix_all.items() if k in ('Wq', 'Wkv', 'Wproj', 'bproj')}
    del _L0_mix_all

    def _L0_ffn_setup():
        import jax, jax.numpy as jnp
        import numpy as np
        NUM_EXPERTS = 8
        TOP_K = 2
        B, S, D = (8, 256, 256)

        def _moe(tokens, router_w, w1, b1, w2, b2):
            N = tokens.shape[0]
            E = router_w.shape[0]
            logits = tokens.astype(jnp.float32) @ router_w.astype(jnp.float32).T
            probs = jax.nn.softmax(logits, axis=-1)
            rw, re = jax.lax.top_k(probs, TOP_K)
            if TOP_K > 1:
                rw = rw / jnp.maximum(rw.sum(-1, keepdims=True), 1e-12)
            rw = rw.astype(tokens.dtype)
            combine = jnp.zeros((N, E), tokens.dtype).at[jnp.arange(N)[:, None], re].set(rw)
            out = tokens
            for e in range(E):
                h = jax.nn.gelu(tokens @ w1[e] + b1[e], approximate=False)
                y = h @ w2[e] + b2[e]
                out = out + combine[:, e:e + 1] * y
            return out
        key = jax.random.key(seed)
        ks = jax.random.split(key, 4)
        scale = 1.0 / np.sqrt(D).astype(np.float32)
        return {'input_embeddings': jax.random.normal(ks[0], (B, S, D), jnp.float32), 'router_w': jax.random.normal(ks[1], (NUM_EXPERTS, D), jnp.float32) * scale, 'w1': jax.random.normal(ks[2], (NUM_EXPERTS, D, D), jnp.float32) * scale, 'b1': jnp.zeros((NUM_EXPERTS, D), jnp.float32), 'w2': jax.random.normal(ks[3], (NUM_EXPERTS, D, D), jnp.float32) * scale, 'b2': jnp.zeros((NUM_EXPERTS, D), jnp.float32)}
    _L0_ffn_all = _L0_ffn_setup()
    _L0_ffn_in = {k: v for k, v in _L0_ffn_all.items() if k in ('router_w', 'w1', 'b1', 'w2', 'b2')}
    del _L0_ffn_all
    return {'x': x, 'src': src, 'dst': dst, 'L0_gnn_w': _L0_gnn_in['w'], 'L0_gnn_W1': _L0_gnn_in['W1'], 'L0_gnn_W2': _L0_gnn_in['W2'], 'L0_gnn_W3': _L0_gnn_in['W3'], 'L0_mix_Wq': _L0_mix_in['Wq'], 'L0_mix_Wkv': _L0_mix_in['Wkv'], 'L0_mix_Wproj': _L0_mix_in['Wproj'], 'L0_mix_bproj': _L0_mix_in['bproj'], 'L0_ffn_router_w': _L0_ffn_in['router_w'], 'L0_ffn_w1': _L0_ffn_in['w1'], 'L0_ffn_b1': _L0_ffn_in['b1'], 'L0_ffn_w2': _L0_ffn_in['w2'], 'L0_ffn_b2': _L0_ffn_in['b2']}

def reference(x, src, dst, L0_gnn_w, L0_gnn_W1, L0_gnn_W2, L0_gnn_W3, L0_mix_Wq, L0_mix_Wkv, L0_mix_Wproj, L0_mix_bproj, L0_ffn_router_w, L0_ffn_w1, L0_ffn_b1, L0_ffn_w2, L0_ffn_b2):
    import jax
    import jax.numpy as jnp

    def _L0_gnn_ref(x, edge_src, edge_dst, w, W1, W2, W3):
        import jax, jax.numpy as jnp
        import numpy as np
        N_NODES = 3125
        N_EDGES = 100000
        D = 256
        agg = jax.ops.segment_sum(x[edge_dst], edge_src, num_segments=N_NODES)
        y = agg + w * x
        h = jax.nn.relu(jnp.einsum('nd,hd->nh', y, W1))
        h = jax.nn.relu(jnp.einsum('nh,gh->ng', h, W2))
        h = jax.nn.relu(jnp.einsum('ng,og->no', h, W3))
        return h + x

    def _L0_mix_ref(x, Wq, Wkv, Wproj, bproj):
        import jax, jax.numpy as jnp
        import numpy as np
        NUM_HEADS = 8
        B, N, C = x.shape
        h = NUM_HEADS
        d = C // h
        q = jnp.einsum('bnc,oc->bno', x, Wq).reshape(B, N, h, d).transpose(0, 2, 1, 3)
        kv = jnp.einsum('bnc,oc->bno', x, Wkv).reshape(B, N, 2, h, d)
        k = kv[:, :, 0].transpose(0, 2, 1, 3)
        v = kv[:, :, 1].transpose(0, 2, 1, 3)
        q = jax.nn.elu(q) + 1.0
        k = jax.nn.elu(k) + 1.0
        k_sum = k.sum(axis=2)
        D_inv = 1.0 / jnp.maximum(jnp.einsum('bhnd,bhd->bhn', q, k_sum), 1e-06)
        context = jnp.einsum('bhnd,bhne->bhde', k, v)
        attn = jnp.einsum('bhnd,bhde->bhne', q, context) * D_inv[..., None]
        out = attn.transpose(0, 2, 1, 3).reshape(B, N, C)
        out = jnp.einsum('bnc,oc->bno', out, Wproj) + bproj
        return out

    def _L0_ffn_ref(input_embeddings, router_w, w1, b1, w2, b2):
        import jax, jax.numpy as jnp
        import numpy as np
        NUM_EXPERTS = 8
        TOP_K = 2
        B, S, D = (8, 256, 256)

        def _moe(tokens, router_w, w1, b1, w2, b2):
            N = tokens.shape[0]
            E = router_w.shape[0]
            logits = tokens.astype(jnp.float32) @ router_w.astype(jnp.float32).T
            probs = jax.nn.softmax(logits, axis=-1)
            rw, re = jax.lax.top_k(probs, TOP_K)
            if TOP_K > 1:
                rw = rw / jnp.maximum(rw.sum(-1, keepdims=True), 1e-12)
            rw = rw.astype(tokens.dtype)
            combine = jnp.zeros((N, E), tokens.dtype).at[jnp.arange(N)[:, None], re].set(rw)
            out = tokens
            for e in range(E):
                h = jax.nn.gelu(tokens @ w1[e] + b1[e], approximate=False)
                y = h @ w2[e] + b2[e]
                out = out + combine[:, e:e + 1] * y
            return out
        b, s, d = input_embeddings.shape
        tokens = input_embeddings.reshape(b * s, d)
        return _moe(tokens, router_w, w1, b1, w2, b2).reshape(b, s, d)
    xn = _layernorm(x, axis=-1)
    x = x + _L0_gnn_ref(xn, src, dst, L0_gnn_w, L0_gnn_W1, L0_gnn_W2, L0_gnn_W3) + _L0_mix_ref(xn[None], L0_mix_Wq, L0_mix_Wkv, L0_mix_Wproj, L0_mix_bproj)[0]
    x = x + _L0_ffn_ref(_layernorm(x, axis=-1)[None], L0_ffn_router_w, L0_ffn_w1, L0_ffn_b1, L0_ffn_w2, L0_ffn_b2)[0]
    return x

_drawn_inputs = setup_inputs


def setup_inputs(seed=0):
    import zlib

    import numpy as np

    out = dict(_drawn_inputs(seed))
    spreads = {'L0_mix_bproj': (0.0, 0.1), 'L0_ffn_b1': (0.0, 0.497), 'L0_ffn_b2': (0.0, 0.336)}
    factors = {'L0_mix_Wq': 8.0, 'L0_mix_Wkv': 8.0, 'L0_mix_Wproj': 8.0}
    for name, (base, spread) in spreads.items():
        noise = np.random.default_rng([zlib.crc32(name.encode()), seed]).standard_normal(out[name].shape)
        drawn = base * np.exp(spread * noise) if base else spread * noise
        out[name] = jnp.asarray(drawn.astype(out[name].dtype))
    for name, factor in factors.items():
        out[name] = (out[name] * factor).astype(out[name].dtype)
    return out
```

```python
from contextlib import ExitStack

import concourse.bass as bass
import concourse.mybir as mybir
from concourse.alu_op_type import AluOpType as ALU

F32, F16, BF16 = mybir.dt.float32, mybir.dt.float16, mybir.dt.bfloat16
I32, U32 = mybir.dt.int32, mybir.dt.uint32
ACT = mybir.ActivationFunctionType
AX_X = mybir.AxisListType.X

N, D = 3125, 256
NE = 53125
TP = 125
NT = N // TP
J = 5
G = NT // J
EC = NE // TP
P = 128
ST = (NE + NT * P) // P
H1, H2 = 64, 32
NX = 8
HD = 32
EPS = 1e-5
RING = 88
OHR = 8
GS = 8
PU = 5
HALF = (EC + 1) // 2
MAGIC = 12582912.0
CA, CB = 3 * TP, 2 * TP
SPAN = [(0, CA), (CA, CA + CB)]
assert ST % RING == 0 and RING % GS == 0 and EC % PU == 0 and ST <= 512


def free2(i, j):
    return i * J if j < 2 else i * J + j - 1


def build(nc, a, out):
    ztab = nc.dram_tensor("ztab", (N, 3 * H1), BF16, kind="Internal").ap()
    with ExitStack() as ctx:
        def sb(name, shape, dt=F32):
            return ctx.enter_context(nc.sbuf_tensor(name, shape, dt))

        def sem(name):
            return ctx.enter_context(nc.semaphore(name))

        bank = [ctx.enter_context(nc.psum_tensor(f"bank{i}", [P, 512], F32)) for i in range(8)]
        m0, m1, h0, h1, y0, y1, agg_ps, lg_ps = bank
        yslot = [b[0:TP, 0:D] for b in (y0, y1, agg_ps, lg_ps)]
        h3slot = [b[0:TP, 0:D] for b in (y0, y1, m0, m1, h0)]
        b2slot = [y0[0:TP, 0:D], y0[0:TP, D:2 * D], y1[0:TP, 0:D], y1[0:TP, D:2 * D], lg_ps[0:TP, 0:D]]

        xb = sb("xb", [TP, NT, D])
        z = sb("z", [TP, NT, H1])

        class Region:

            def __init__(self, name, words):
                self.t, self.at, self.words = sb(name, [P, words]), 0, words

            def restart(self):
                self.at = 0
                return self

            def take(self, rows, n, dt=F32):
                words = n if dt in (F32, I32) else (n + 1) // 2
                v = self.t[0:rows, self.at:self.at + words]
                self.at += words
                assert self.at <= self.words
                return v if dt == F32 else v.bitcast(dt)[:, 0:n]

        r = Region("region_xn", NT * D)
        xnT_all = r.take(P, NT * 2 * TP)
        r.restart()
        tT = r.take(P, 2 * J * TP).rearrange("p (k n) -> p k n", k=2)
        hT = r.take(P, 4 * J * TP).rearrange("p (s f n) -> p s f n", s=2, f=2)
        h1T = r.take(H1, J * TP)
        h2T = r.take(H2, J * TP)
        combT = r.take(NX, J * TP)

        r = Region("region_buckets", NT * EC + 1)
        flat_boh = r.take(TP, NT * EC, F16)
        flat_cnt = r.take(TP, NT * EC, F16)
        boh = flat_boh.rearrange("p (b c) -> p b c", b=NT)
        cnt = flat_cnt.rearrange("p (b c) -> p b c", b=NT)
        r.restart()
        qT = r.take(P, 2 * N).rearrange("p (k n) -> p k n", k=2)
        x2 = r.take(TP, J * D).rearrange("p (j d) -> p j d", j=J)
        tk = r.take(TP, J * D).rearrange("p (j d) -> p j d", j=J)
        acc = r.take(TP, J * D).rearrange("p (j d) -> p j d", j=J)

        r = Region("region_rows", RING * 3 * H1 // 2)
        prod = r.take(TP, NT * HALF).rearrange("p (b c) -> p b c", b=NT)
        xn = r.take(TP, J * D).rearrange("p (j d) -> p j d", j=J)
        r.restart()
        rows = r.take(P, RING * 3 * H1, BF16).rearrange("p (r s h) -> p r s h", r=RING, s=3)

        r = Region("region_w1", NX * 2 * D)
        zparts = r.take(TP, NT * 3 * H1, BF16).rearrange("p (t s h) -> p t s h", t=NT, s=3)
        zrest = r.take(TP, NT * H1).rearrange("p (t h) -> p t h", t=NT)
        r.restart()
        w1 = r.take(P, NX * 2 * D).rearrange("p (e k f) -> p e k f", e=NX, k=2)

        r = Region("region_w2", NX * 2 * D)
        src = r.take(TP, EC, I32)
        dst = r.take(TP, EC, I32)
        rnd = r.take(TP, EC)
        tile_of = r.take(TP, EC, F16)
        local = r.take(TP, EC)
        val1 = r.take(TP, EC)
        odd = r.take(TP, EC)
        val2 = r.take(TP, EC)
        pos = r.take(TP, EC)
        place_row, place_col = local, odd
        r.restart()
        w2 = r.take(P, NX * 2 * D).rearrange("p (e k f) -> p e k f", e=NX, k=2)

        r = Region("region_steps", 2080)
        moh = r.take(TP, PU * ST, F16).rearrange("p (u n) -> p u n", u=PU)
        soh = r.take(TP, PU * 2 * P, F16).rearrange("p (u v n) -> p u v n", u=PU, v=2)
        r.restart()
        kb = r.take(TP, 2 * D).rearrange("p (s d) -> p s d", s=2)
        vb = r.take(TP, 2 * D).rearrange("p (s d) -> p s d", s=2)
        ek = r.take(TP, 2 * D).rearrange("p (s d) -> p s d", s=2)
        eq = r.take(P, 4 * TP).rearrange("p (s k n) -> p s k n", s=2, k=2)
        r.restart()
        mctx = r.take(P, 2 * P).rearrange("p (c n) -> p c n", c=2)
        den = r.take(P, 4 * TP).rearrange("p (s n) -> p s n", s=2)
        qn = r.take(P, 4 * TP).rearrange("p (s n) -> p s n", s=2)
        hs = r.take(TP, J * H1).rearrange("p (j h) -> p j h", j=J)
        noh = r.take(P, OHR * TP, BF16).rearrange("p (r n) -> p r n", r=OHR)
        xnT = sb("xnT", [P, J, 2, TP])

        wq = sb("wq", [P, 2, D])
        wkv = sb("wkv", [P, 2, 2 * D])
        wp = sb("wp", [P, 2, D])
        w1g = sb("w1g", [P, 2, H1])
        w2g = sb("w2g", [H1, H2])
        w3g = sb("w3g", [H2, D])
        rw = sb("rw", [P, 2, NX])
        b1 = sb("b1", [P, NX, 2])
        b2 = sb("b2", [NX, D])
        bp = sb("bp", [TP, D])
        wself = sb("wself", [TP, 1])

        ident = sb("ident", [P, P])
        before = sb("before", [TP, TP])
        ones = sb("ones", [TP, TP])
        same_head = sb("same_head", [P, P])
        zeros = sb("zeros", [P, 512], BF16)
        iota_col = sb("iota_col", [TP, ST], F16)
        iota_row = sb("iota_row", [TP, P], F16)
        iota_node = sb("iota_node", [P, TP], BF16)
        iota_x = sb("iota_x", [TP, J, NX])
        epsc = sb("epsc", [TP, 1])

        stats = sb("stats", [TP, NT, 6])
        mv = sb("mv", [TP, NT, 2])
        std = sb("std", [TP, NT])
        rstd = sb("rstd", [TP, NT])
        shift = sb("shift", [TP, NT])

        edges_of = sb("edges_of", [TP, NT])
        tiles_of = sb("tiles_of", [TP, NT])
        tile_end = sb("tile_end", [TP, NT])
        tile_start = sb("tile_start", [TP, NT])
        adj = sb("adj", [TP, NT])
        bounds = sb("bounds", [TP, 2, NT], I32)
        slot_odd = sb("slot_odd", [P, ST])
        slot_dst = sb("slot_dst", [P, ST], I32)
        slot_src = sb("slot_src", [P, ST])
        now_dst = sb("now_dst", [P, RING], I32)

        mout = sb("mout", [P, 2, D])
        ksum = sb("ksum", [P, 2])
        ksb = sb("ksb", [P, 2, P])

        stats2 = sb("stats2", [TP, J, 6])
        mv2 = sb("mv2", [TP, J, 2])
        std2 = sb("std2", [TP, J])
        rstd2 = sb("rstd2", [TP, J])
        shift2 = sb("shift2", [TP, J])
        lg = sb("lg", [TP, J, NX])
        top = sb("top", [TP, J, NX])
        top_at = sb("top_at", [TP, J, NX], U32)
        top_atf = sb("top_atf", [TP, J, NX])
        ex = sb("ex", [TP, J, NX])
        exs = sb("exs", [TP, J])
        pw = sb("pw", [TP, J, 2])
        pws = sb("pws", [TP, J])
        pick = sb("pick", [TP, 2, J, NX])
        comb = sb("comb", [TP, J, NX])

        edges_in, x_in, gnn_in, mix_in, ffn_in, wx_in = map(sem, (
            "edges_in", "x_in", "gnn_in", "mix_in", "ffn_in", "wx_in"))
        pool_set, pool_step, dve_step, act_step = map(sem, ("pool_set", "pool_step", "dve_step", "act_step"))
        stats_done, std_done, shift_done, xn_done = map(sem, ("stats_done", "std_done", "shift_done", "xn_done"))
        t1_ready, t1_copied, z_ready, z_copied = map(sem, ("t1_ready", "t1_copied", "z_ready", "z_copied"))
        zparts_done, ztab_stored, xb_done = map(sem, ("zparts_done", "ztab_stored", "xb_done"))
        counts_ready, totals_ready, oh_ready, oh_used, placed, slots_done, bounds_done = map(sem, (
            "counts_ready", "totals_ready", "oh_ready", "oh_used", "placed", "slots_done", "bounds_done"))
        xnT_kept, xn_added, xnT_back, kvq_ready, ek_done, eq_done, k_done, q_done, ctx_used = map(sem, (
            "xnT_kept", "xn_added", "xnT_back", "kvq_ready", "ek_done", "eq_done", "k_done", "q_done", "ctx_used"))
        ctx_ready, ctx_masked, mout_ready, mout_done = map(sem, (
            "ctx_ready", "ctx_masked", "mout_ready", "mout_done"))
        gsem = [sem(f"gather{k}") for k in range(GS)]
        gathered, noh_ready, tile_used, agg_ready = map(sem, ("gathered", "noh_ready", "tile_used", "agg_ready"))
        den_ready, den_read, qn_done, mix_ready, mix_added = map(sem, (
            "den_ready", "den_read", "qn_done", "mix_ready", "mix_added"))
        hs_done, g1_ready, g1_done, g2_ready, g2_done, g3_ready, x2_done = map(sem, (
            "hs_done", "g1_ready", "g1_done", "g2_ready", "g2_done", "g3_ready", "x2_done"))
        var2_done, std2_done, tk_done, t3_ready, tT_done = map(sem, (
            "var2_done", "std2_done", "tk_done", "t3_ready", "tT_done"))
        lg_ready, top_done, ex_done, comb_done, ct_ready, ct_done, b2_ready, acc_set = map(sem, (
            "lg_ready", "top_done", "ex_done", "comb_done", "ct_ready", "ct_done", "b2_ready", "acc_set"))
        h_ready, h_done, y_ready, y_read, stored = map(sem, ("h_ready", "h_done", "y_ready", "y_read", "stored"))

        passed = sem("passed")

        block = ctx.enter_context(nc.Block())

        @block.sync
        def _(sp):
            sp.dma_start(src, a["src"].rearrange("(p c) -> p c", p=TP)).then_inc(edges_in, 16)
            sp.dma_start(dst, a["dst"].rearrange("(p c) -> p c", p=TP)).then_inc(edges_in, 16)
            sp.dma_start(xb[:], a["x"].rearrange("(t p) d -> p t d", p=TP)).then_inc(x_in, 16)
            sp.dma_start(w1g[:], a["W1T"].rearrange("(k p) h -> p k h", p=P)).then_inc(gnn_in, 16)
            sp.dma_start(wself[:], a["w"].rearrange("(a b) -> a b", a=1).to_broadcast([TP, 1])).then_inc(gnn_in, 16)
            sp.dma_start(w2g[:], a["W2T"]).then_inc(gnn_in, 16)
            sp.dma_start(w3g[:], a["W3T"]).then_inc(gnn_in, 16)
            sp.dma_start(bp[:], a["bp"].rearrange("(a d) -> a d", a=1).to_broadcast([TP, D])).then_inc(mix_in, 16)
            sp.dma_start(wq[:], a["WqT"].rearrange("(k p) h -> p k h", p=P)).then_inc(mix_in, 16)
            sp.dma_start(wkv[:], a["WkvT"].rearrange("(k p) h -> p k h", p=P)).then_inc(mix_in, 16)
            sp.dma_start(wp[:], a["WpT"].rearrange("(k p) h -> p k h", p=P)).then_inc(mix_in, 16)
            sp.dma_start(rw[:], a["rT"].rearrange("(k p) h -> p k h", p=P)).then_inc(ffn_in, 16)
            sp.dma_start(b1[:], a["b1T"].rearrange("p (e k) -> p e k", e=NX)).then_inc(ffn_in, 16)
            sp.dma_start(b2[:], a["b2"]).then_inc(ffn_in, 16)
            sp.wait_ge(zparts_done, 1)
            sp.dma_start(ztab.rearrange("(t p) h -> p t h", p=TP),
                         zparts.rearrange("p t s h -> p t (s h)")).then_inc(ztab_stored, 16)
            sp.wait_ge(ztab_stored, 16)
            sp.dma_start(w1, a["w1"].rearrange("e (k p) f -> p e k f", p=P)).then_inc(wx_in, 16)
            sp.wait_ge(placed, 1)
            sp.dma_start(w2, a["w2"].rearrange("e (k p) f -> p e k f", p=P)).then_inc(wx_in, 16)
            with sp.Fori(0, G) as i:
                sp.wait_ge(y_read, (i + 1) * NX * J)
                sp.dma_start(out.rearrange("(g j p) d -> g p j d", p=TP, j=J)[bass.ds(i, 1), :, :, :]
                             .rearrange("g p j d -> p (g j) d"), acc).then_inc(stored, 16)
                sp.wait_ge(stored, (i + 1) * 16)
                sp.sem_inc(passed, 1)

        @block.gpsimd
        def _(pool):
            nc.gpsimd.memset(ident[:], 0.0).then_inc(pool_step, 1)
            nc.gpsimd.memset(before[:], 1.0).then_inc(pool_step, 1)
            nc.gpsimd.memset(same_head[:], 1.0).then_inc(pool_step, 1)
            nc.gpsimd.memset(ones[:], 1.0)
            nc.gpsimd.memset(zeros[:], 0.0)
            nc.gpsimd.memset(epsc[:], EPS)
            nc.gpsimd.iota(iota_col[:], [[1, ST]], base=0, channel_multiplier=0,
                           allow_small_or_imprecise_dtypes=True)
            nc.gpsimd.iota(iota_row[:], [[1, P]], base=0, channel_multiplier=0,
                           allow_small_or_imprecise_dtypes=True)
            nc.gpsimd.iota(iota_node[:], [[1, TP]], base=1, channel_multiplier=0,
                           allow_small_or_imprecise_dtypes=True)
            nc.gpsimd.iota(iota_x[:], [[0, J], [1, NX]], base=0, channel_multiplier=0,
                           allow_small_or_imprecise_dtypes=True)
            pool.wait_ge(pool_step, 3)
            nc.gpsimd.affine_select(out=ident[:], in_=ident[:], compare_op=ALU.not_equal, fill=1.0, base=0,
                                    pattern=[[-1, P]], channel_multiplier=1)
            nc.gpsimd.affine_select(out=before[:], in_=before[:], compare_op=ALU.is_gt, fill=0.0, base=0,
                                    pattern=[[1, TP]], channel_multiplier=-1)
            blocks = same_head[:].rearrange("p (b c) -> p b c", c=HD)
            nc.gpsimd.affine_select(out=blocks, in_=blocks, compare_op=ALU.is_ge, fill=0.0, base=0,
                                    pattern=[[-HD, P // HD], [0, HD]], channel_multiplier=1).then_inc(pool_step, 1)
            pool.wait_ge(pool_step, 4)
            nc.gpsimd.affine_select(out=blocks, in_=blocks, compare_op=ALU.is_ge, fill=0.0, base=HD - 1,
                                    pattern=[[HD, P // HD], [0, HD]], channel_multiplier=-1).then_inc(pool_set, 1)

            pool.wait_ge(mix_in, 64)
            with pool.Fori(0, G) as i:
                pool.wait_ge(t1_copied, (i + 1) * J)
                nc.gpsimd.tensor_copy(xnT_all[:, bass.ds(i * (J * 2 * TP), J * 2 * TP)],
                                      xnT[:].rearrange("p j k n -> p (j k n)")).then_inc(xnT_kept, 1)
                here = xb[:, bass.ds(i * J, J), :]
                nc.gpsimd.tensor_tensor(here, here, xn, ALU.add).then_inc(xn_added, 1)
                pool.wait_ge(xn_added, i + 1)
                pool.sem_inc(passed, 1)
                nc.gpsimd.tensor_tensor(here, here, bp[:].rearrange("p (a d) -> p a d", a=1).to_broadcast([TP, J, D]),
                                        ALU.add).then_inc(xb_done, 1)

            pool.wait_ge(z_copied, NT)
            nc.gpsimd.tensor_copy(zparts[:, :, 0, :], z[:]).then_inc(pool_step, 1)
            pool.wait_ge(pool_step, 5)
            nc.gpsimd.tensor_tensor(zrest, z[:], zparts[:, :, 0, :], ALU.subtract).then_inc(pool_step, 1)
            pool.wait_ge(pool_step, 6)
            nc.gpsimd.tensor_copy(zparts[:, :, 1, :], zrest).then_inc(pool_step, 1)
            pool.wait_ge(pool_step, 7)
            nc.gpsimd.tensor_tensor(zparts[:, :, 2, :], zrest, zparts[:, :, 1, :],
                                    ALU.subtract).then_inc(zparts_done, 1)

            pool.wait_ge(slots_done, 1)
            pool.wait_ge(ztab_stored, 16)
            with pool.Fori(0, ST // RING) as i:
                uses = RING // GS
                for k in range(GS):
                    pool.wait_ge(gsem[k], i * (16 * uses))
                nc.gpsimd.tensor_copy(now_dst[:], slot_dst[:, bass.ds(i * RING, RING)]).then_inc(pool_step, 1)
                pool.wait_ge(pool_step, i + 8)
                for u in range(RING):
                    k, n = u % GS, u // GS
                    pool.wait_ge(gsem[k], i * (16 * uses) + 16 * n)
                    pool.wait_ge(tile_used, i * RING + (u + 1))
                    pool.sem_inc(gathered, 1)
                    nc.gpsimd.indirect_dma_start(
                        rows[:, u, :, :].rearrange("p s h -> p (s h)"), None, ztab,
                        bass.IndirectOffsetOnAxis(now_dst[:, u:u + 1], 0)).then_inc(gsem[k], 16)
            for k in range(GS):
                pool.wait_ge(gsem[k], 16 * ST // GS)
                pool.sem_inc(gathered, 1)

        @block.scalar
        def _(act):
            act.wait_ge(pool_set, 1)
            act.wait_ge(stats_done, 1)
            nc.scalar.activation(std[:], mv[:, :, 1], ACT.Sqrt, bias=epsc[:]).then_inc(std_done, 1)
            act.wait_ge(shift_done, 1)
            with act.Fori(0, G) as i:
                act.wait_ge(xn_added, i)
                act.wait_ge(xnT_kept, i)
                for j in range(J):
                    t = i * J + j
                    nc.scalar.activation(xn[:, j, :], xb[:, bass.ds(t, 1), :].rearrange("p a d -> p (a d)"),
                                         ACT.Identity, scale=rstd[:, bass.ds(t, 1)],
                                         bias=shift[:, bass.ds(t, 1)]).then_inc(xn_done, 1)
                for j in range(J):
                    t, s = i * J + j, j % 2
                    act.wait_ge(t1_ready, t + 1)
                    nc.scalar.copy(xnT[:, j, :, :], (m0, m1)[s][:, 0:CB].rearrange("p (k n) -> p k n", k=2)
                                   ).then_inc(t1_copied, 1)
                    act.wait_ge(z_ready, t + 1)
                    nc.scalar.copy(z[:, bass.ds(t, 1), :].rearrange("p a h -> p (a h)"),
                                   (h0, h1)[s][0:TP, 0:H1]).then_inc(z_copied, 1)

            with act.Fori(0, G) as i:
                for j in range(J):
                    t, s = i * J + j, j % 2
                    act.wait_ge(kvq_ready, t + 1)
                    act.wait_ge(ctx_used, free2(i, j))
                    act.wait_ge(q_done, free2(i, j))
                    kv = (y0, y1)[s]
                    qp = (m0, m1)[s][:, 0:CB].rearrange("p (k n) -> p k n", k=2)
                    nc.scalar.activation(ek[:, s, :], kv[0:TP, 0:D], ACT.Relu, scale=-1.0).then_inc(act_step, 1)
                    nc.scalar.copy(vb[:, s, :], kv[0:TP, D:2 * D])
                    nc.scalar.activation(eq[:, s, :, :], qp, ACT.Relu, scale=-1.0).then_inc(act_step, 1)
                    act.wait_ge(act_step, t * 2 + 1)
                    nc.scalar.activation(ek[:, s, :], ek[:, s, :], ACT.Exp, scale=-1.0).then_inc(ek_done, 1)
                    act.wait_ge(act_step, t * 2 + 2)
                    nc.scalar.activation(eq[:, s, :, :], eq[:, s, :, :], ACT.Exp, scale=-1.0).then_inc(eq_done, 1)
            for c in range(2):
                act.wait_ge(mout_ready, c + 1)
                nc.scalar.copy(mout[:, c, :], (m0, m1)[c][:, 0:D]).then_inc(mout_done, 1)

            with act.Fori(0, G) as i:
                act.wait_ge(g1_ready, i + 1)
                nc.scalar.activation(h1T[:, 0:CA], m0[0:H1, 0:CA], ACT.Relu)
                nc.scalar.activation(h1T[:, CA:CA + CB], m1[0:H1, 0:CB], ACT.Relu).then_inc(g1_done, 1)
                act.wait_ge(g2_ready, i + 1)
                nc.scalar.activation(h2T[:, 0:CA], h0[0:H2, 0:CA], ACT.Relu)
                nc.scalar.activation(h2T[:, CA:CA + CB], h1[0:H2, 0:CB], ACT.Relu).then_inc(g2_done, 1)
                act.wait_ge(var2_done, i + 1)
                nc.scalar.activation(std2[:], mv2[:, :, 1], ACT.Sqrt, bias=epsc[:]).then_inc(std2_done, 1)
                act.wait_ge(t3_ready, i + 1)
                for k, (pa, pb) in enumerate(((m0, m1), (h0, h1))):
                    nc.scalar.copy(tT[:, k, 0:CA], pa[:, 0:CA])
                    last = nc.scalar.copy(tT[:, k, CA:CA + CB], pb[:, 0:CB])
                last.then_inc(tT_done, 1)
                act.wait_ge(top_done, i + 1)
                nc.scalar.activation(ex[:], ex[:], ACT.Exp).then_inc(ex_done, 1)
                act.wait_ge(ct_ready, i + 1)
                nc.scalar.copy(combT[:, 0:CA], m0[0:NX, 0:CA])
                nc.scalar.copy(combT[:, CA:CA + CB], m1[0:NX, 0:CB]).then_inc(ct_done, 1)
                for e in range(NX):
                    if e >= 2:
                        act.wait_ge(y_ready, i * (NX * J) + (e - 1) * J)
                    for f in range(2):
                        act.wait_ge(h_ready, i * (2 * NX) + 2 * e + f + 1)
                        pa, pb = ((m0, m1), (h0, h1))[f]
                        nc.scalar.activation(hT[:, e % 2, f, 0:CA], pa[:, 0:CA], ACT.Gelu, bias=b1[:, e, f:f + 1])
                        nc.scalar.activation(hT[:, e % 2, f, CA:CA + CB], pb[:, 0:CB], ACT.Gelu,
                                             bias=b1[:, e, f:f + 1]).then_inc(h_done, 1)

        @block.vector
        def _(dve):
            step = [0]

            def link(ins):
                step[0] += 1
                ins.then_inc(dve_step, 1)
                dve.wait_ge(dve_step, step[0])

            dve.wait_ge(edges_in, 32)
            link(nc.vector.tensor_scalar(rnd, src, 1.0 / TP, 0.5 / TP - 0.5, ALU.mult, ALU.add))
            link(nc.vector.tensor_scalar(tile_of, rnd, MAGIC, -MAGIC, ALU.add, ALU.add))
            nc.vector.scalar_tensor_tensor(local, tile_of, -float(TP), src, ALU.mult, ALU.add)
            link(nc.vector.tensor_scalar(rnd, dst, 0.5, -0.25, ALU.mult, ALU.add))
            link(nc.vector.tensor_scalar(val1, rnd, MAGIC, -MAGIC, ALU.add, ALU.add))
            link(nc.vector.scalar_tensor_tensor(odd, val1, -2.0, dst, ALU.mult, ALU.add))
            link(nc.vector.tensor_scalar(odd, odd, float(P), 1.0, ALU.mult, ALU.add))
            nc.vector.tensor_tensor(val2, odd, local, ALU.add)
            for b in range(NT):
                last = nc.vector.tensor_scalar(boh[:, b, :], tile_of, float(b), None, ALU.is_equal)
            link(last)

            dve.wait_ge(x_in, 16)
            for t in range(NT):
                last = nc.vector.bn_stats(stats[:, t, :], xb[:, t, :])
            link(last)
            for t in range(NT):
                last = nc.vector.bn_aggr(mv[:, t, :], stats[:, t, :])
            last.then_inc(stats_done, 1)
            dve.wait_ge(std_done, 1)
            link(nc.vector.reciprocal(rstd[:], std[:]))
            nc.vector.scalar_tensor_tensor(shift[:], mv[:, :, 0], -1.0, rstd[:], ALU.mult,
                                           ALU.mult).then_inc(shift_done, 1)

            link(nc.vector.tensor_tensor_scan(flat_cnt, flat_boh, flat_boh, 0.0, ALU.add, ALU.max))
            end = cnt[:, :, EC - 1]
            nc.vector.tensor_copy(edges_of[:, 0:1], end[:, 0:1])
            nc.vector.tensor_tensor(edges_of[:, 1:NT], end[:, 1:NT], end[:, 0:NT - 1],
                                    ALU.subtract).then_inc(counts_ready, 1)
            dve.wait_ge(totals_ready, 1)
            above, total = lg_ps[0:TP, 0:NT], lg_ps[0:TP, NT:2 * NT]
            link(nc.vector.tensor_scalar(tiles_of[:], total, 1.0 / P, 0.5 - 0.5 / P, ALU.mult, ALU.add))
            link(nc.vector.tensor_scalar(tiles_of[:], tiles_of[:], MAGIC, -MAGIC, ALU.add, ALU.add))
            link(nc.vector.tensor_scalar(tiles_of[:], tiles_of[:], 1.0, None, ALU.max))
            link(nc.vector.tensor_tensor_scan(tile_end[:], tiles_of[:], tiles_of[:], 0.0, ALU.add, ALU.max))
            link(nc.vector.tensor_tensor(tile_start[:], tile_end[:], tiles_of[:], ALU.subtract))
            nc.vector.tensor_copy(bounds[:, 0, :], tile_start[:])
            nc.vector.tensor_copy(bounds[:, 1, :], tile_end[:]).then_inc(bounds_done, 1)
            link(nc.vector.scalar_tensor_tensor(adj[:], tile_start[:], float(P), above, ALU.mult, ALU.add))
            link(nc.vector.tensor_scalar(adj[:], adj[:], -1.0, None, ALU.add))
            link(nc.vector.tensor_tensor(adj[:, 1:NT], adj[:, 1:NT], end[:, 0:NT - 1], ALU.subtract))
            for c0, c1 in ((0, HALF), (HALF, EC)):
                w = c1 - c0
                for b in range(NT):
                    last = nc.vector.scalar_tensor_tensor(prod[:, b, 0:w], cnt[:, b, c0:c1], adj[:, b:b + 1],
                                                          boh[:, b, c0:c1], ALU.add, ALU.mult)
                link(last)
                link(nc.vector.tensor_reduce(pos[:, c0:c1], prod[:, :, 0:w].rearrange("p b c -> p c b"),
                                             AX_X, ALU.add))
            link(nc.vector.tensor_scalar(rnd, pos, 1.0 / P, 0.5 / P - 0.5, ALU.mult, ALU.add))
            link(nc.vector.tensor_scalar(place_col, rnd, MAGIC, -MAGIC, ALU.add, ALU.add))
            link(nc.vector.scalar_tensor_tensor(place_row, place_col, -float(P), pos, ALU.mult, ALU.add))

            dve.wait_ge(pool_set, 1)
            with dve.Fori(0, EC // PU) as i:
                for u in range(PU):
                    c = i * PU + u
                    col = bass.ds(c, 1)
                    dve.wait_ge(oh_used, c + 1)
                    nc.vector.tensor_scalar(moh[:, u, :], iota_col[:], place_col[:, col], None, ALU.is_equal)
                    nc.vector.tensor_scalar(soh[:, u, 0, :], iota_row[:], place_row[:, col], val1[:, col],
                                            ALU.is_equal, ALU.mult)
                    nc.vector.tensor_scalar(soh[:, u, 1, :], iota_row[:], place_row[:, col], val2[:, col],
                                            ALU.is_equal, ALU.mult).then_inc(oh_ready, 1)

            dve.wait_ge(placed, 1)
            got1, got2 = h0[:, 0:ST], h1[:, 0:ST]
            link(nc.vector.tensor_scalar(slot_odd[:], got2, float(P), None, ALU.is_ge))
            nc.vector.scalar_tensor_tensor(slot_dst[:], got1, 2.0, slot_odd[:], ALU.mult, ALU.add)
            nc.vector.scalar_tensor_tensor(slot_src[:], slot_odd[:], -float(P), got2, ALU.mult,
                                           ALU.add).then_inc(slots_done, 1)
            dve.wait_ge(slots_done, 1)

            dve.wait_ge(xnT_kept, G)
            with dve.Fori(0, G) as i:
                dve.wait_ge(kvq_ready, i * J)
                nc.vector.tensor_copy(xnT[:].rearrange("p j k n -> p (j k n)"),
                                      xnT_all[:, bass.ds(i * (J * 2 * TP), J * 2 * TP)]).then_inc(xnT_back, 1)
                for j in range(J):
                    t, s = i * J + j, j % 2
                    dve.wait_ge(ctx_used, free2(i, j))
                    dve.wait_ge(ek_done, t + 1)
                    nc.vector.scalar_tensor_tensor(kb[:, s, :], (y0, y1)[s][0:TP, 0:D], 0.0, ek[:, s, :],
                                                   ALU.max, ALU.add).then_inc(k_done, 1)
                    dve.wait_ge(eq_done, t + 1)
                    nc.vector.scalar_tensor_tensor(
                        qT[:, :, bass.ds(t * TP, TP)], (m0, m1)[s][:, 0:CB].rearrange("p (k n) -> p k n", k=2),
                        0.0, eq[:, s, :, :], ALU.max, ALU.add).then_inc(q_done, 1)
            dve.wait_ge(ctx_ready, 1)
            for c in range(2):
                nc.vector.tensor_tensor(mctx[:, c, :], lg_ps[:, c * P:(c + 1) * P], same_head[:], ALU.mult)
            link(nc.vector.tensor_copy(ksum[:], lg_ps[:, 2 * P:2 * P + 2]))
            for c in range(2):
                last = nc.vector.tensor_scalar(ksb[:, c, :], same_head[:], ksum[:, c:c + 1], None, ALU.mult)
            last.then_inc(ctx_masked, 1)

            def mix_add(i, j):
                t = i * J + j
                dve.wait_ge(mix_ready, t + 1)
                dve.wait_ge(xb_done, G)
                here = xb[:, bass.ds(t, 1), :].rearrange("p a d -> p (a d)")
                nc.vector.tensor_tensor(here, here, yslot[j % 2], ALU.add).then_inc(mix_added, 1)
                if j == J - 1:
                    dve.wait_ge(mix_added, (i + 1) * J)

            link0 = step[0]

            with dve.Fori(0, G) as i:
                n = [0]

                def chain(ins):
                    n[0] += 1
                    ins.then_inc(dve_step, 1)
                    dve.wait_ge(dve_step, i * CHAIN + (link0 + n[0]))

                for j in range(J):
                    t, s = i * J + j, j % 2
                    dve.wait_ge(den_ready, t + 1)
                    dve.wait_ge(mix_ready, free2(i, j))
                    nc.vector.tensor_scalar(den[:, s, :], (m0, m1)[s][:, 0:CB], 1e-6, None,
                                            ALU.max).then_inc(den_read, 1)
                    dve.wait_ge(den_read, t + 1)
                    chain(nc.vector.reciprocal(den[:, s, :], den[:, s, :]))
                    nc.vector.tensor_tensor(
                        qn[:, s, :].rearrange("p (k n) -> p k n", k=2), den[:, s, :].rearrange("p (k n) -> p k n", k=2),
                        qT[:, :, bass.ds(t * TP, TP)], ALU.mult).then_inc(qn_done, 1)
                    if j >= 1:
                        mix_add(i, j - 1)
                mix_add(i, J - 1)

                for j in range(J):
                    b = i * J + j
                    t0 = dve.value_load(bounds[0:1, 0, bass.ds(b, 1)], min_val=0, max_val=ST)
                    t1 = dve.value_load(bounds[0:1, 1, bass.ds(b, 1)], min_val=1, max_val=ST)
                    with dve.Fori(t0, t1) as t:
                        dve.wait_ge(tile_used, t + (1 + RING - OHR))
                        nc.vector.tensor_scalar(noh[:, bass.ds(t % OHR, 1), :].rearrange("p a n -> p (a n)"),
                                                iota_node[:], slot_src[:, bass.ds(t, 1)], None,
                                                ALU.is_equal).then_inc(noh_ready, 1)
                dve.wait_ge(agg_ready, i + 1)
                nc.vector.scalar_tensor_tensor(
                    hs, z[:, bass.ds(i * J, J), :], wself[:, 0:1],
                    agg_ps[0:TP, 0:J * H1].rearrange("p (j h) -> p j h", j=J), ALU.mult, ALU.add).then_inc(hs_done, 1)
                dve.wait_ge(xb_done, G)
                for j in range(J):
                    dve.wait_ge(g3_ready, i * J + j + 1)
                    h3 = h3slot[j]
                    chain(nc.vector.scalar_tensor_tensor(
                        x2[:, j, :], h3, 0.0, xb[:, bass.ds(i * J + j, 1), :].rearrange("p a d -> p (a d)"),
                        ALU.max, ALU.add))
                    nc.vector.bn_stats(stats2[:, j, :], x2[:, j, :]).then_inc(x2_done, 1)
                dve.wait_ge(x2_done, i * J + J)
                dve.sem_inc(passed, 1)
                for j in range(J):
                    last = nc.vector.bn_aggr(mv2[:, j, :], stats2[:, j, :])
                last.then_inc(var2_done, 1)
                dve.wait_ge(std2_done, i + 1)
                chain(nc.vector.reciprocal(rstd2[:], std2[:]))
                chain(nc.vector.scalar_tensor_tensor(shift2[:], mv2[:, :, 0], -1.0, rstd2[:], ALU.mult, ALU.mult))
                for j in range(J):
                    last = nc.vector.tensor_scalar(tk[:, j, :], x2[:, j, :], rstd2[:, j:j + 1], shift2[:, j:j + 1],
                                                   ALU.mult, ALU.add)
                last.then_inc(tk_done, 1)
                dve.wait_ge(tk_done, i + 1)
                dve.wait_ge(stored, i * 16)
                chain(nc.vector.tensor_tensor(acc, x2, tk, ALU.add))

                dve.wait_ge(lg_ready, i + 1)
                chain(nc.vector.tensor_copy(lg[:].rearrange("p j x -> p (j x)"), lg_ps[0:TP, 0:J * NX]))
                dve.sem_inc(passed, 1)
                for j in range(J):
                    last = nc.vector.max(top[:, j, :], lg[:, j, :])
                chain(last)
                dve.sem_inc(passed, 1)
                for j in range(J):
                    nc.vector.max_index(top_at[:, j, :], top[:, j, :], lg[:, j, :])
                nc.vector.tensor_tensor(ex[:], top[:], top[:, :, 0:1].to_broadcast([TP, J, NX]),
                                        ALU.subtract).then_inc(top_done, 1)
                dve.wait_ge(top_done, i + 1)
                chain(nc.vector.tensor_copy(top_atf[:], top_at[:]))
                dve.wait_ge(ex_done, i + 1)
                chain(nc.vector.tensor_reduce(exs[:], ex[:], AX_X, ALU.add))
                chain(nc.vector.reciprocal(exs[:], exs[:]))
                chain(nc.vector.tensor_tensor(pw[:], ex[:, :, 0:2],
                                              exs[:].rearrange("p (j a) -> p j a", a=1).to_broadcast([TP, J, 2]),
                                              ALU.mult))
                chain(nc.vector.tensor_tensor(pws[:], pw[:, :, 0], pw[:, :, 1], ALU.add))
                chain(nc.vector.tensor_scalar(pws[:], pws[:], 1e-12, None, ALU.max))
                chain(nc.vector.reciprocal(pws[:], pws[:]))
                chain(nc.vector.tensor_tensor(pw[:], pw[:],
                                              pws[:].rearrange("p (j a) -> p j a", a=1).to_broadcast([TP, J, 2]),
                                              ALU.mult))
                for r2 in range(2):
                    last = nc.vector.tensor_tensor(pick[:, r2, :, :], iota_x[:],
                                                   top_atf[:, :, r2:r2 + 1].to_broadcast([TP, J, NX]), ALU.is_equal)
                chain(last)
                for r2 in range(2):
                    last = nc.vector.tensor_tensor(pick[:, r2, :, :], pick[:, r2, :, :],
                                                   pw[:, :, r2:r2 + 1].to_broadcast([TP, J, NX]), ALU.mult)
                chain(last)
                nc.vector.tensor_tensor(comb[:], pick[:, 0, :, :], pick[:, 1, :, :], ALU.add).then_inc(comb_done, 1)
                for j in range(J):
                    dve.wait_ge(b2_ready, i * J + (2, 2, 4, 4, 5)[j])
                    last = nc.vector.tensor_tensor(acc[:, j, :], acc[:, j, :], b2slot[j], ALU.add).then_inc(acc_set, 1)
                dve.wait_ge(acc_set, (i + 1) * J)
                for e in range(NX):
                    for j in range(J):
                        q = e * J + j
                        dve.wait_ge(y_ready, i * (NX * J) + q + 1)
                        if e > 0:
                            dve.wait_ge(y_read, i * (NX * J) + q - J + 1)
                        nc.vector.scalar_tensor_tensor(acc[:, j, :], yslot[q % 4], comb[:, j, e:e + 1], acc[:, j, :],
                                                       ALU.mult, ALU.add).then_inc(y_read, 1)
                assert n[0] == CHAIN, n[0]

        @block.tensor
        def _(pe):
            def zero(ps, start):
                w = ps.shape[-1]
                return nc.tensor.matmul(ps, zeros[:, 0:ps.shape[0]], zeros[:, 0:w], start=start, stop=not start,
                                        skip_group_check=True)

            pe.sem_inc(oh_used, PU)
            pe.sem_inc(tile_used, RING)
            pe.wait_ge(pool_set, 1)

            pe.wait_ge(gnn_in, 64)
            with pe.Fori(0, G) as i:
                for j in range(J):
                    t, s = i * J + j, j % 2
                    pe.wait_ge(xn_done, t + 1)
                    pe.wait_ge(t1_copied, free2(i, j))
                    for k in range(2):
                        last = nc.tensor.transpose((m0, m1)[s][:, k * TP:(k + 1) * TP],
                                                   xn[:, j, k * P:(k + 1) * P], ident[0:TP, 0:TP])
                    last.then_inc(t1_ready, 1)
                    pe.wait_ge(t1_copied, t + 1)
                    pe.wait_ge(z_copied, free2(i, j))
                    for k in range(2):
                        last = nc.tensor.matmul((h0, h1)[s][0:TP, 0:H1], xnT[:, j, k, :], w1g[:, k, :],
                                                start=(k == 0), stop=(k == 1))
                    last.then_inc(z_ready, 1)

            pe.wait_ge(counts_ready, 1)
            nc.tensor.matmul(lg_ps[0:TP, 0:NT], before[:], edges_of[:], start=True, stop=True)
            nc.tensor.matmul(lg_ps[0:TP, NT:2 * NT], ones[:], edges_of[:], start=True, stop=True
                             ).then_inc(totals_ready, 1)

            got = (h0[:, 0:ST], h1[:, 0:ST])
            pe.wait_ge(z_copied, NT)
            for v in range(2):
                zero(got[v], True)
            with pe.Fori(0, EC // PU) as i:
                for u in range(PU):
                    pe.wait_ge(oh_ready, i * PU + (u + 1))
                    for v in range(2):
                        last = nc.tensor.matmul(got[v], soh[:, u, v, :], moh[:, u, :], start=False, stop=False,
                                                skip_group_check=True)
                    last.then_inc(oh_used, 1)
            zero(got[0], False)
            zero(got[1], False).then_inc(placed, 1)

            pe.wait_ge(mix_in, 64)
            nctx = 2 * P + 2
            zero(lg_ps[:, 0:nctx], True)

            def context(i, j):
                s = j % 2
                pe.wait_ge(k_done, i * J + j + 1)
                for c in range(2):
                    f = slice(c * P, (c + 1) * P)
                    nc.tensor.matmul(lg_ps[:, f], vb[:, s, f], kb[:, s, f], start=False, stop=False,
                                     skip_group_check=True)
                    last = nc.tensor.matmul(lg_ps[:, 2 * P + c:2 * P + c + 1], kb[:, s, f], ones[:, 0:1],
                                            start=False, stop=False, skip_group_check=True)
                last.then_inc(ctx_used, 1)

            with pe.Fori(0, G) as i:
                pe.wait_ge(xnT_back, i + 1)
                for j in range(J):
                    t, s = i * J + j, j % 2
                    pe.wait_ge(k_done, free2(i, j))
                    pe.wait_ge(q_done, free2(i, j))            
                    kv = (y0, y1)[s][0:TP, 0:2 * D]
                    for k in range(2):
                        nc.tensor.matmul(kv, xnT[:, j, k, :], wkv[:, k, :], start=(k == 0), stop=(k == 1))
                    for c in range(2):
                        for k in range(2):
                            last = nc.tensor.matmul((m0, m1)[s][:, c * TP:(c + 1) * TP],
                                                    wq[:, k, c * P:(c + 1) * P], xnT[:, j, k, :],
                                                    start=(k == 0), stop=(k == 1))
                    last.then_inc(kvq_ready, 1)
                    if j >= 1:
                        context(i, j - 1)
                context(i, J - 1)
            zero(lg_ps[:, 0:nctx], False).then_inc(ctx_ready, 1)
            pe.wait_ge(ctx_masked, 1)
            for c in range(2):
                nc.tensor.matmul((m0, m1)[c][:, 0:D], mctx[:, c, :], wp[:, c, :], start=True, stop=True
                                 ).then_inc(mout_ready, 1)
            pe.wait_ge(mout_done, 2)

            with pe.Fori(0, G) as i:
                def denominators(j):
                    for c in range(2):
                        last = nc.tensor.matmul((m0, m1)[j % 2][:, c * TP:(c + 1) * TP], ksb[:, c, :],
                                                qT[:, c, bass.ds((i * J + j) * TP, TP)], start=True, stop=True)
                    last.then_inc(den_ready, 1)

                pe.wait_ge(y_read, i * (NX * J))
                denominators(0)
                for j in range(J):
                    s = j % 2
                    if j + 1 < J:
                        if j >= 1:
                            pe.wait_ge(den_read, i * J + j)
                        denominators(j + 1)
                    pe.wait_ge(qn_done, i * J + j + 1)
                    pe.wait_ge(mix_added, free2(i, j))
                    for c in range(2):
                        last = nc.tensor.matmul(yslot[j % 2], qn[:, s, c * TP:(c + 1) * TP], mout[:, c, :],
                                                start=(c == 0), stop=(c == 1))
                    last.then_inc(mix_ready, 1)

                for j in range(J):
                    b = i * J + j
                    t0 = pe.value_load(bounds[0:1, 0, bass.ds(b, 1)], min_val=0, max_val=ST)
                    t1 = pe.value_load(bounds[0:1, 1, bass.ds(b, 1)], min_val=1, max_val=ST)
                    agg = agg_ps[0:TP, j * H1:(j + 1) * H1]
                    zero(agg, True)
                    with pe.Fori(t0, t1) as t:
                        pe.wait_ge(gathered, t + (1 + GS))
                        pe.wait_ge(noh_ready, t + 1)
                        for part in range(3):
                            last = nc.tensor.matmul(
                                agg, noh[:, bass.ds(t % OHR, 1), :].rearrange("p a n -> p (a n)"),
                                rows[:, bass.ds(t % RING, 1), part, :].rearrange("p a h -> p (a h)"),
                                start=False, stop=False, skip_group_check=True)
                        last.then_inc(tile_used, 1)
                    last = zero(agg, False)
                last.then_inc(agg_ready, 1)

                pe.wait_ge(hs_done, i + 1)
                pe.wait_ge(mix_added, (i + 1) * J)
                pe.sem_inc(passed, 1)
                for j in range(J):
                    ps = m0[0:H1, j * TP:(j + 1) * TP] if j < 3 else m1[0:H1, (j - 3) * TP:(j - 2) * TP]
                    last = nc.tensor.transpose(ps, hs[:, j, :], ident[0:TP, 0:TP])
                last.then_inc(g1_ready, 1)
                pe.wait_ge(g1_done, i + 1)
                pe.sem_inc(passed, 1)
                for (lo, hi), ps in zip(SPAN, (h0, h1)):
                    last = nc.tensor.matmul(ps[0:H2, 0:hi - lo], w2g[:], h1T[:, lo:hi], start=True, stop=True)
                last.then_inc(g2_ready, 1)
                pe.wait_ge(g2_done, i + 1)
                for j in range(J):
                    nc.tensor.matmul(h3slot[j], h2T[:, j * TP:(j + 1) * TP], w3g[:],
                                     start=True, stop=True).then_inc(g3_ready, 1)

                pe.wait_ge(tk_done, i + 1)
                for k, (pa, pb) in enumerate(((m0, m1), (h0, h1))):
                    for j in range(J):
                        ps = pa[:, j * TP:(j + 1) * TP] if j < 3 else pb[:, (j - 3) * TP:(j - 2) * TP]
                        last = nc.tensor.transpose(ps, tk[:, j, k * P:(k + 1) * P], ident[0:TP, 0:TP])
                last.then_inc(t3_ready, 1)
                pe.wait_ge(ffn_in, 48)
                pe.wait_ge(tT_done, i + 1)
                for j in range(J):
                    for k in range(2):
                        last = nc.tensor.matmul(lg_ps[0:TP, j * NX:(j + 1) * NX], tT[:, k, j * TP:(j + 1) * TP],
                                                rw[:, k, :], start=(k == 0), stop=(k == 1))
                last.then_inc(lg_ready, 1)
                pe.wait_ge(comb_done, i + 1)
                for j in range(J):
                    ps = m0[0:NX, j * TP:(j + 1) * TP] if j < 3 else m1[0:NX, (j - 3) * TP:(j - 2) * TP]
                    last = nc.tensor.transpose(ps, comb[:, j, :], ident[0:TP, 0:TP])
                last.then_inc(ct_ready, 1)
                pe.wait_ge(ct_done, i + 1)
                for j in range(J):
                    nc.tensor.matmul(b2slot[j], combT[:, j * TP:(j + 1) * TP], b2[:],
                                     start=True, stop=True).then_inc(b2_ready, 1)

                pe.wait_ge(wx_in, 32)

                def first_layer(e):
                    for f in range(2):
                        if e >= 1:
                            pe.wait_ge(h_done, i * (2 * NX) + 2 * (e - 1) + f + 1)
                        for (lo, hi), ps in zip(SPAN, ((m0, m1), (h0, h1))[f]):
                            for k in range(2):
                                last = nc.tensor.matmul(ps[:, 0:hi - lo], w1[:, e, k, f * P:(f + 1) * P],
                                                        tT[:, k, lo:hi], start=(k == 0), stop=(k == 1))
                        last.then_inc(h_ready, 1)

                first_layer(0)
                for e in range(NX):
                    if e + 1 < NX:
                        first_layer(e + 1)
                    pe.wait_ge(h_done, i * (2 * NX) + 2 * e + 2)
                    for j in range(J):
                        q = e * J + j
                        if q < 4:
                            pe.wait_ge(acc_set, (i + 1) * J)
                        else:
                            pe.wait_ge(y_read, i * (NX * J) + q - 3)
                        for f in range(2):
                            last = nc.tensor.matmul(yslot[q % 4], hT[:, e % 2, f, j * TP:(j + 1) * TP],
                                                    w2[:, e, f, :], start=(f == 0), stop=(f == 1))
                        last.then_inc(y_ready, 1)


CHAIN = 25


def kernel(**inputs):
    import numpy as np
    import concourse.bacc as bacc
    from concourse.bass_utils import run_bass_kernel_spmd

    g = {k: np.asarray(v) for k, v in inputs.items()}
    arrays = {
        "x": g["x"], "src": g["src"], "dst": g["dst"], "w": g["L0_gnn_w"],
        "W1T": g["L0_gnn_W1"].T, "W2T": g["L0_gnn_W2"].T, "W3T": g["L0_gnn_W3"].T,
        "WqT": g["L0_mix_Wq"].T, "WkvT": g["L0_mix_Wkv"].T, "WpT": g["L0_mix_Wproj"].T,
        "bp": g["L0_mix_bproj"], "rT": g["L0_ffn_router_w"].T,
        "w1": g["L0_ffn_w1"], "w2": g["L0_ffn_w2"], "b2": g["L0_ffn_b2"],
        "b1T": g["L0_ffn_b1"].reshape(NX * 2, P).T,
    }
    arrays = {k: np.ascontiguousarray(v) for k, v in arrays.items()}
    nc = bacc.Bacc("TRN2", target_bir_lowering=False, num_devices=1)
    a = {k: nc.dram_tensor(f"in_{k}", v.shape, mybir.dt.from_np(v.dtype), kind="ExternalInput").ap()
         for k, v in arrays.items()}
    out = nc.dram_tensor("out", (N, D), F32, kind="ExternalOutput").ap()
    build(nc, a, out)
    r = run_bass_kernel_spmd(nc, [{f"in_{k}": v for k, v in arrays.items()}], core_ids=[0])
    return r.results[0]["out"]
```

```python
from contextlib import ExitStack

import concourse.bass as bass
import concourse.mybir as mybir
from concourse.alu_op_type import AluOpType as ALU

F32, F16, BF16 = mybir.dt.float32, mybir.dt.float16, mybir.dt.bfloat16
I32, U32 = mybir.dt.int32, mybir.dt.uint32
ACT = mybir.ActivationFunctionType
AX_X = mybir.AxisListType.X

N, D = 3125, 256
NE = 53125
TP = 125
NT = N // TP
J = 5
G = NT // J
EC = NE // TP
P = 128
BT = 18
ST = NT * BT
H1, H2 = 64, 32
NX = 8
HD = 32
EPS = 1e-5
PU = 5
BATCHES = EC // PU
OB = 4
HALF = (EC + 1) // 2
MAGIC = 12582912.0
CA, CB = 3 * TP, 2 * TP
SPAN = [(0, CA), (CA, CA + CB)]
NOWHERE = 600.0
SPILL_BANKS = [(0, 7), (7, 13), (13, 19), (19, 25)]
assert EC % PU == 0 and BATCHES % OB == 1 and NT % 2 == 1 and ST <= 512


def build(nc, a, out):
    ztab = nc.dram_tensor("ztab", (N, 3 * H1), BF16, kind="Internal").ap()
    with ExitStack() as ctx:
        def sb(name, shape, dt=F32):
            return ctx.enter_context(nc.sbuf_tensor(name, shape, dt))

        def sem(name):
            return ctx.enter_context(nc.semaphore(name))

        bank = [ctx.enter_context(nc.psum_tensor(f"bank{i}", [P, 512], F32)) for i in range(8)]
        m0, m1, h0, h1, y0, y1, agg_ps, lg_ps = bank
        yslot = [b[0:TP, 0:D] for b in (y0, y1, lg_ps)]
        h3slot = [b[0:TP, 0:D] for b in (y0, y1, m0, m1, h0)]
        b2slot = [y0[0:TP, 0:D], y0[0:TP, D:2 * D], y1[0:TP, 0:D], y1[0:TP, D:2 * D], lg_ps[0:TP, 0:D]]

        xb = sb("xb", [TP, NT, D])
        z = sb("z", [TP, NT, H1])

        class Region:

            def __init__(self, name, words):
                self.t, self.at, self.words = sb(name, [P, words]), 0, words

            def restart(self):
                self.at = 0
                return self

            def take(self, rows, n, dt=F32):
                words = n if dt in (F32, I32) else (n + 1) // 2
                v = self.t[0:rows, self.at:self.at + words]
                self.at += words
                assert self.at <= self.words
                return v if dt == F32 else v.bitcast(dt)[:, 0:n]

        r = Region("region_xn", NT * D)
        xnT_all = r.take(P, NT * 2 * TP)
        r.restart()
        tT = r.take(P, 2 * J * TP).rearrange("p (k n) -> p k n", k=2)
        hT = r.take(P, 4 * J * TP).rearrange("p (s f n) -> p s f n", s=2, f=2)
        h1T = r.take(H1, J * TP)
        h2T = r.take(H2, J * TP)
        combT = r.take(NX, J * TP)

        r = Region("region_buckets", NT * EC + 1)
        flat_boh = r.take(TP, NT * EC, F16)
        flat_cnt = r.take(TP, NT * EC, F16)
        boh = flat_boh.rearrange("p (b c) -> p b c", b=NT)
        cnt = flat_cnt.rearrange("p (b c) -> p b c", b=NT)
        r.restart()
        moh = r.take(TP, OB * PU * ST, F16).rearrange("p (b u n) -> p b u n", b=OB, u=PU)
        eqh = r.take(TP, OB * P * PU, F16).rearrange("p (b n u) -> p b n u", b=OB, u=PU)
        soh1 = r.take(TP, OB * P * PU, F16).rearrange("p (b u n) -> p b u n", b=OB, u=PU)
        soh2 = r.take(TP, OB * P * PU, F16).rearrange("p (b n u) -> p b n u", b=OB, u=PU)
        r.restart()
        x2 = r.take(TP, J * D).rearrange("p (j d) -> p j d", j=J)
        tk = r.take(TP, J * D).rearrange("p (j d) -> p j d", j=J)
        acc = r.take(TP, J * D).rearrange("p (j d) -> p j d", j=J)
        mctx = r.take(P, 2 * P).rearrange("p (c n) -> p c n", c=2)
        eq = r.take(P, 4 * TP).rearrange("p (s n) -> p s n", s=2)
        qp = r.take(P, 4 * TP).rearrange("p (s n) -> p s n", s=2)
        den = r.take(P, 4 * TP).rearrange("p (s n) -> p s n", s=2)
        qn = r.take(P, 4 * TP).rearrange("p (s n) -> p s n", s=2)
        hs = r.take(TP, J * H1).rearrange("p (j h) -> p j h", j=J)
        noh = r.take(P, 2 * TP * BT, BF16).rearrange("p (s n c) -> p s n c", s=2, c=BT)

        r = Region("region_rows", J * BT * 3 * H1 // 2)
        prod = r.take(TP, NT * HALF).rearrange("p (b c) -> p b c", b=NT)
        xn = r.take(TP, 2 * D).rearrange("p (s d) -> p s d", s=2)
        kb = r.take(TP, 2 * D).rearrange("p (s d) -> p s d", s=2)
        vb = r.take(TP, 2 * D).rearrange("p (s d) -> p s d", s=2)
        ek = r.take(TP, 2 * D).rearrange("p (s d) -> p s d", s=2)
        r.restart()
        spill_rows = r.take(TP, 3 * H1, BF16).rearrange("p (s h) -> p s h", s=3)
        spill_rhs = r.take(TP, 3 * NT * H1, BF16).rearrange("p (s b h) -> p s b h", s=3, b=NT)
        spill_oh = r.take(TP, TP, BF16)
        spill_in = r.take(TP, NT, BF16)
        spill_dst = r.take(TP, 1, I32)
        r.restart()
        rows = r.take(P, J * BT * 3 * H1, BF16).rearrange("p (r s h) -> p r s h", r=J * BT, s=3)

        r = Region("region_w1", NX * 2 * D)
        zparts = r.take(TP, NT * 3 * H1, BF16).rearrange("p (t s h) -> p t s h", t=NT, s=3)
        zrest = r.take(TP, NT * H1).rearrange("p (t h) -> p t h", t=NT)
        r.restart()
        w1 = r.take(P, NX * 2 * D).rearrange("p (e k f) -> p e k f", e=NX, k=2)

        r = Region("region_w2", NX * 2 * D)
        src = r.take(TP, EC, I32)
        dst = r.take(TP, EC, I32)
        rnd = r.take(TP, EC)
        tile_of = r.take(TP, EC, F16)
        local = r.take(TP, EC)
        val1 = r.take(TP, EC)
        odd = r.take(TP, EC)
        val2 = r.take(TP, EC, F16)
        pos = r.take(TP, EC)
        place_row = r.take(TP, EC, F16)
        spilled = r.take(TP, EC)
        place_col = odd
        spill_tile = pos
        r.restart()
        w2 = r.take(P, NX * 2 * D).rearrange("p (e k f) -> p e k f", e=NX, k=2)

        xnT = sb("xnT", [P, 2, 2, TP])

        wq = sb("wq", [P, 2, D])
        wkv = sb("wkv", [P, 2, 2 * D])
        wp = sb("wp", [P, 2, D])
        w1g = sb("w1g", [P, 2, H1])
        w2g = sb("w2g", [H1, H2])
        w3g = sb("w3g", [H2, D])
        rw = sb("rw", [P, 2, NX])
        b1 = sb("b1", [P, NX, 2])
        b2 = sb("b2", [NX, D])
        bp = sb("bp", [1, D])
        wself = sb("wself", [TP, 1])

        ident = sb("ident", [P, P])
        before = sb("before", [TP, TP])
        ones = sb("ones", [TP, TP])
        same_head = sb("same_head", [P, P])
        zeros = sb("zeros", [P, 512], BF16)
        iota_col = sb("iota_col", [TP, ST], F16)
        iota_row = sb("iota_row", [TP, P, PU], F16)
        iota_flat = sb("iota_flat", [TP, P], F16)
        iota_node = sb("iota_node", [P, TP, BT], BF16)
        iota_x = sb("iota_x", [TP, J, NX])
        epsc = sb("epsc", [TP, 1])

        stats = sb("stats", [TP, NT, 6])
        mv = sb("mv", [TP, NT, 2])
        std = sb("std", [TP, NT])
        rstd = sb("rstd", [TP, NT])
        shift = sb("shift", [TP, NT])

        edges_of = sb("edges_of", [TP, NT])
        adj = sb("adj", [TP, NT])
        fullest = sb("fullest", [TP, 1])
        spill = sb("spill", [TP, 1], I32)
        slot_odd = sb("slot_odd", [P, ST])
        slot_dst = sb("slot_dst", [P, ST], I32)
        slot_src = sb("slot_src", [P, ST], BF16)
        now_dst = sb("now_dst", [P, J * BT], I32)

        mout = sb("mout", [P, 2, D])
        ksum = sb("ksum", [P, 2])
        ksb = sb("ksb", [P, 2, P])

        stats2 = sb("stats2", [TP, J, 6])
        mv2 = sb("mv2", [TP, J, 2])
        std2 = sb("std2", [TP, J])
        rstd2 = sb("rstd2", [TP, J])
        shift2 = sb("shift2", [TP, J])
        lg = sb("lg", [TP, J, NX])
        top = sb("top", [TP, J, NX])
        top_at = sb("top_at", [TP, J, NX], U32)
        top_atf = sb("top_atf", [TP, J, NX])
        ex = sb("ex", [TP, J, NX])
        exs = sb("exs", [TP, J])
        pw = sb("pw", [TP, J, 2])
        pws = sb("pws", [TP, J])
        pick = sb("pick", [TP, 2, J, NX])
        comb = sb("comb", [TP, J, NX])

        edges_in, gnn_in, mix_in, ffn_in, wx_in = map(sem, ("edges_in", "gnn_in", "mix_in", "ffn_in", "wx_in"))
        x_in = [sem(f"x_in{g}") for g in range(G)]
        pool_set, pool_step, dve_step, act_step = map(sem, ("pool_set", "pool_step", "dve_step", "act_step"))
        stats_done, std_done, shift_done, xn_done = map(sem, ("stats_done", "std_done", "shift_done", "xn_done"))
        t1_ready, t1_copied, z_ready, z_copied = map(sem, ("t1_ready", "t1_copied", "z_ready", "z_copied"))
        zpart0_done, zrest_done, zpart1_done, zparts_done, ztab_stored = map(sem, (
            "zpart0_done", "zrest_done", "zpart1_done", "zparts_done", "ztab_stored"))
        counts_ready, totals_ready, eqh_ready, moh_ready, oh_ready, oh2_ready, oh_used, placed, slots_done = map(sem, (
            "counts_ready", "totals_ready", "eqh_ready", "moh_ready", "oh_ready", "oh2_ready", "oh_used", "placed", "slots_done"))
        spill_known, spill_landed, spill_ready, spill_summed, spill_total, spill_added, values_free = map(sem, (
            "spill_known", "spill_landed", "spill_ready", "spill_summed", "spill_total", "spill_added",
            "values_free"))
        spill_step = sem("spill_step")
        xnT_kept, xn_added, kv_ready, kv_read, ek_done, k_done, ctx_used = map(sem, (
            "xnT_kept", "xn_added", "kv_ready", "kv_read", "ek_done", "k_done", "ctx_used"))
        ctx_ready, ctx_masked, mout_ready, mout_done = map(sem, (
            "ctx_ready", "ctx_masked", "mout_ready", "mout_done"))
        q_ready, eq_done, qp_done, den_ready, den_read, den_inv, qn_done, mix_ready, mix_added = map(sem, (
            "q_ready", "eq_done", "qp_done", "den_ready", "den_read", "den_inv", "qn_done", "mix_ready",
            "mix_added"))
        landed = [sem(f"landed{j}") for j in range(J)]
        noh_ready, bucket_used = map(sem, ("noh_ready", "bucket_used"))
        hs_done, g1_ready, g1_done, g2_ready, g2_done, g3_ready, x2_done = map(sem, (
            "hs_done", "g1_ready", "g1_done", "g2_ready", "g2_done", "g3_ready", "x2_done"))
        var2_done, std2_done, tk_done, t3_ready, tT_done = map(sem, (
            "var2_done", "std2_done", "tk_done", "t3_ready", "tT_done"))
        lg_ready, top_done, ex_done, comb_done, ct_ready, ct_done, b2_ready, acc_set = map(sem, (
            "lg_ready", "top_done", "ex_done", "comb_done", "ct_ready", "ct_done", "b2_ready", "acc_set"))
        h_ready, h_done, y_ready, y_read, stored = map(sem, ("h_ready", "h_done", "y_ready", "y_read", "stored"))

        dst_copied = sem("dst_copied")
        passed = sem("passed")

        def tile(x, t):
            return x[:, bass.ds(t, 1), :].rearrange("p a d -> p (a d)")

        def columns(v, n, w):
            return v[:, bass.ds(n * PU, PU)].rearrange("p (a u) -> p a u", a=1).to_broadcast([TP, w, PU])

        block = ctx.enter_context(nc.Block())

        @block.sync
        def _(sp):
            sp.sem_inc(stored, 16)
            sp.dma_start(src, a["src"].rearrange("(p c) -> p c", p=TP)).then_inc(edges_in, 16)
            sp.dma_start(dst, a["dst"].rearrange("(p c) -> p c", p=TP)).then_inc(edges_in, 16)
            for g in range(G):
                sp.dma_start(xb[:, g * J:(g + 1) * J, :],
                             a["x"].rearrange("(g t p) d -> g p t d", p=TP, g=G)[g]).then_inc(x_in[g], 16)
            sp.dma_start(w1g[:], a["W1T"].rearrange("(k p) h -> p k h", p=P)).then_inc(gnn_in, 16)
            sp.dma_start(wself[:], a["w"].rearrange("(a b) -> a b", a=1).to_broadcast([TP, 1])).then_inc(gnn_in, 16)
            sp.dma_start(w2g[:], a["W2T"]).then_inc(gnn_in, 16)
            sp.dma_start(w3g[:], a["W3T"]).then_inc(gnn_in, 16)
            sp.dma_start(wkv[:], a["WkvT"].rearrange("(k p) h -> p k h", p=P)).then_inc(mix_in, 16)
            sp.dma_start(wq[:], a["WqT"].rearrange("(k p) h -> p k h", p=P)).then_inc(mix_in, 16)
            sp.dma_start(wp[:], a["WpT"].rearrange("(k p) h -> p k h", p=P)).then_inc(mix_in, 16)
            sp.dma_start(bp[:], a["bp"].rearrange("(a d) -> a d", a=1)).then_inc(mix_in, 16)
            sp.dma_start(rw[:], a["rT"].rearrange("(k p) h -> p k h", p=P)).then_inc(ffn_in, 16)
            sp.dma_start(b1[:], a["b1T"].rearrange("p (e k) -> p e k", e=NX)).then_inc(ffn_in, 16)
            sp.dma_start(b2[:], a["b2"]).then_inc(ffn_in, 16)
            sp.wait_ge(zparts_done, 1)
            sp.dma_start(ztab.rearrange("(t p) h -> p t h", p=TP),
                         zparts.rearrange("p t s h -> p t (s h)")).then_inc(ztab_stored, 16)
            sp.wait_ge(ztab_stored, 16)
            sp.dma_start(w1, a["w1"].rearrange("e (k p) f -> p e k f", p=P)).then_inc(wx_in, 16)
            sp.wait_ge(values_free, 1)
            sp.dma_start(w2, a["w2"].rearrange("e (k p) f -> p e k f", p=P)).then_inc(wx_in, 16)
            with sp.Fori(0, G) as i:
                sp.wait_ge(y_read, (i + 1) * NX * J)
                sp.dma_start(out.rearrange("(g j p) d -> g p j d", p=TP, j=J)[bass.ds(i, 1), :, :, :]
                             .rearrange("g p j d -> p (g j) d"), acc).then_inc(stored, 16)
                sp.wait_ge(stored, (i + 2) * 16)
                sp.sem_inc(passed, 1)

        @block.gpsimd
        def _(pool):
            nc.gpsimd.memset(ident[:], 0.0).then_inc(pool_step, 1)
            nc.gpsimd.memset(before[:], 1.0).then_inc(pool_step, 1)
            nc.gpsimd.memset(same_head[:], 1.0).then_inc(pool_step, 1)
            nc.gpsimd.memset(ones[:], 1.0)
            nc.gpsimd.memset(zeros[:], 0.0)
            nc.gpsimd.memset(epsc[:], EPS)
            nc.gpsimd.iota(iota_col[:], [[1, ST]], base=0, channel_multiplier=0,
                           allow_small_or_imprecise_dtypes=True)
            nc.gpsimd.iota(iota_row[:], [[1, P], [0, PU]], base=0, channel_multiplier=0,
                           allow_small_or_imprecise_dtypes=True)
            nc.gpsimd.iota(iota_flat[:], [[1, P]], base=0, channel_multiplier=0,
                           allow_small_or_imprecise_dtypes=True)
            nc.gpsimd.iota(iota_node[:], [[1, TP], [0, BT]], base=1, channel_multiplier=0,
                           allow_small_or_imprecise_dtypes=True)
            nc.gpsimd.iota(iota_x[:], [[0, J], [1, NX]], base=0, channel_multiplier=0,
                           allow_small_or_imprecise_dtypes=True)
            pool.wait_ge(pool_step, 3)
            nc.gpsimd.affine_select(out=ident[:], in_=ident[:], compare_op=ALU.not_equal, fill=1.0, base=0,
                                    pattern=[[-1, P]], channel_multiplier=1)
            nc.gpsimd.affine_select(out=before[:], in_=before[:], compare_op=ALU.is_gt, fill=0.0, base=0,
                                    pattern=[[1, TP]], channel_multiplier=-1)
            blocks = same_head[:].rearrange("p (b c) -> p b c", c=HD)
            nc.gpsimd.affine_select(out=blocks, in_=blocks, compare_op=ALU.is_ge, fill=0.0, base=0,
                                    pattern=[[-HD, P // HD], [0, HD]], channel_multiplier=1).then_inc(pool_step, 1)
            pool.wait_ge(pool_step, 4)
            nc.gpsimd.affine_select(out=blocks, in_=blocks, compare_op=ALU.is_ge, fill=0.0, base=HD - 1,
                                    pattern=[[HD, P // HD], [0, HD]], channel_multiplier=-1).then_inc(pool_set, 1)

            pool.sem_inc(xn_added, 2)
            pool.sem_inc(xnT_kept, 2)

            def attention_in(t, s):
                pool.wait_ge(xn_done, t + 1)
                pool.sem_inc(passed, 1)
                nc.gpsimd.tensor_tensor(tile(xb, t), tile(xb, t), xn[:, s, :], ALU.add).then_inc(xn_added, 1)
                pool.wait_ge(t1_copied, t + 3)
                nc.gpsimd.tensor_copy(xnT_all[:, bass.ds(t * (2 * TP), 2 * TP)],
                                      xnT[:, s, :, :].rearrange("p k n -> p (k n)")).then_inc(xnT_kept, 1)
                pool.wait_ge(ek_done, t + 1)
                nc.gpsimd.tensor_tensor(kb[:, s, :], kb[:, s, :], ek[:, s, :], ALU.add).then_inc(k_done, 1)

            with pool.Fori(0, NT // 2) as i:
                for s in range(2):
                    attention_in(i * 2 + s, s)
            attention_in(NT - 1, 0)

            def second_value(n, b):
                pool.wait_ge(eqh_ready, n + 1)
                pool.sem_inc(passed, 1)
                nc.gpsimd.tensor_tensor(soh2[:, b, :, :], eqh[:, b, :, :], columns(val2, n, P), ALU.mult
                                        ).then_inc(oh2_ready, 1)

            with pool.Fori(0, BATCHES // OB) as i:
                for b in range(OB):
                    second_value(i * OB + b, b)
            second_value(BATCHES - 1, 0)

            pool.wait_ge(ztab_stored, 16)
            pool.wait_ge(spill_known, 1)
            with pool.If(pool.value_load(spill[0:1, 0:1], min_val=0, max_val=1) > 0):
                with pool.Fori(0, EC) as c:
                    pool.wait_ge(spill_summed, c + 1)
                    nc.gpsimd.tensor_copy(spill_dst, dst[:, bass.ds(c, 1)]).then_inc(pool_step, 1)
                    pool.wait_ge(pool_step, c + 5)
                    pool.sem_inc(passed, 1)
                    nc.gpsimd.indirect_dma_start(
                        spill_rows.rearrange("p s h -> p (s h)"), None, ztab,
                        bass.IndirectOffsetOnAxis(spill_dst, 0)).then_inc(spill_landed, 16)
                pool.wait_ge(spill_added, 1)

            pool.wait_ge(slots_done, 1)
            with pool.Fori(0, G) as i:
                for j in range(J):
                    pool.wait_ge(bucket_used, i * J + (j + 1))
                    here = slice(j * BT, (j + 1) * BT)
                    nc.gpsimd.tensor_copy(now_dst[:, here],
                                          slot_dst[:, bass.ds(i * (J * BT) + j * BT, BT)]).then_inc(dst_copied, 1)
                    pool.wait_ge(dst_copied, i * J + (j + 1))
                    pool.sem_inc(passed, 1)
                    for u in range(j * BT, (j + 1) * BT):
                        nc.gpsimd.indirect_dma_start(
                            rows[:, u, :, :].rearrange("p s h -> p (s h)"), None, ztab,
                            bass.IndirectOffsetOnAxis(now_dst[:, u:u + 1], 0)).then_inc(landed[j], 16)
            for j in range(J):
                pool.wait_ge(landed[j], 16 * BT * G)

        @block.scalar
        def _(act):
            act.wait_ge(pool_set, 1)
            act.wait_ge(stats_done, 1)
            nc.scalar.activation(std[:], mv[:, :, 1], ACT.Sqrt, bias=epsc[:]).then_inc(std_done, 1)
            act.wait_ge(shift_done, 1)

            def normalize(t, s):
                act.wait_ge(xn_added, t + 1)
                nc.scalar.activation(xn[:, s, :], tile(xb, t), ACT.Identity, scale=rstd[:, bass.ds(t, 1)],
                                     bias=shift[:, bass.ds(t, 1)]).then_inc(xn_done, 1)

            def copy_transposed(t, s):
                act.wait_ge(t1_ready, t + 1)
                act.wait_ge(kv_ready, t + 1)
                act.wait_ge(xnT_kept, t + 1)
                nc.scalar.copy(xnT[:, s, :, :], (m0, m1)[s][:, 0:CB].rearrange("p (k n) -> p k n", k=2)
                               ).then_inc(t1_copied, 1)

            def copy_z(t, s):
                act.wait_ge(z_ready, t + 1)
                nc.scalar.copy(tile(z, t), (h0, h1)[s][0:TP, 0:H1]).then_inc(z_copied, 1)

            def k_and_v(t, s):
                kv = (y0, y1)[s]
                act.wait_ge(kv_ready, t + 3)
                act.wait_ge(ctx_used, t + 1)
                nc.scalar.activation(ek[:, s, :], kv[0:TP, 0:D], ACT.Relu, scale=-1.0).then_inc(act_step, 1)
                nc.scalar.activation(kb[:, s, :], kv[0:TP, 0:D], ACT.Relu)
                nc.scalar.copy(vb[:, s, :], kv[0:TP, D:2 * D]).then_inc(kv_read, 1)
                act.wait_ge(act_step, t + 1)
                nc.scalar.activation(ek[:, s, :], ek[:, s, :], ACT.Exp, scale=-1.0).then_inc(ek_done, 1)

            act.sem_inc(t1_copied, 2)
            act.sem_inc(z_copied, 2)
            act.sem_inc(kv_read, 2)
            normalize(0, 0)
            normalize(1, 1)
            copy_transposed(0, 0)

            def step(t, s):
                copy_transposed(t + 1, 1 - s)
                normalize(t + 2, s)
                copy_z(t, s)
                k_and_v(t, s)

            step(0, 0)
            with act.Fori(0, NT // 2 - 1) as i:
                step(i * 2 + 1, 1)
                step(i * 2 + 2, 0)
            copy_transposed(NT - 1, 0)
            copy_z(NT - 2, 1)
            k_and_v(NT - 2, 1)
            copy_z(NT - 1, 0)
            k_and_v(NT - 1, 0)

            act.wait_ge(z_copied, NT + 2)
            nc.scalar.copy(zparts[:, :, 0, :], z[:]).then_inc(zpart0_done, 1)

            def first_value(n, b):
                act.wait_ge(eqh_ready, n + 1)
                for u in range(PU):
                    last = nc.scalar.activation(soh1[:, b, u, :], eqh[:, b, :, u], ACT.Copy,
                                                scale=val1[:, bass.ds(n * PU + u, 1)])
                last.then_inc(oh_ready, 1)

            with act.Fori(0, BATCHES // OB // 2) as i:
                for b in range(OB):
                    first_value(i * OB + b, b)
            act.wait_ge(zrest_done, 1)
            nc.scalar.copy(zparts[:, :, 1, :], zrest).then_inc(zpart1_done, 1)
            with act.Fori(BATCHES // OB // 2, BATCHES // OB) as i:
                for b in range(OB):
                    first_value(i * OB + b, b)
            first_value(BATCHES - 1, 0)

            for c in range(2):
                act.wait_ge(mout_ready, c + 1)
                nc.scalar.copy(mout[:, c, :], (m0, m1)[c][:, 0:D]).then_inc(mout_done, 1)

            def q_half(t, s):
                act.wait_ge(q_ready, t + 1)
                act.wait_ge(qp_done, t + 1)
                nc.scalar.activation(eq[:, s, :], (m0, m1)[s][:, 0:CB], ACT.Relu, scale=-1.0).then_inc(act_step, 1)
                act.wait_ge(act_step, t + (NT + 1))
                nc.scalar.activation(eq[:, s, :], eq[:, s, :], ACT.Exp, scale=-1.0).then_inc(eq_done, 1)

            with act.Fori(0, NT // 2) as i:
                for s in range(2):
                    q_half(i * 2 + s, s)
            q_half(NT - 1, 0)

            with act.Fori(0, G) as i:
                act.wait_ge(g1_ready, i + 1)
                nc.scalar.activation(h1T[:, 0:CA], m0[0:H1, 0:CA], ACT.Relu)
                nc.scalar.activation(h1T[:, CA:CA + CB], m1[0:H1, 0:CB], ACT.Relu).then_inc(g1_done, 1)
                act.wait_ge(g2_ready, i + 1)
                nc.scalar.activation(h2T[:, 0:CA], h0[0:H2, 0:CA], ACT.Relu)
                nc.scalar.activation(h2T[:, CA:CA + CB], h1[0:H2, 0:CB], ACT.Relu).then_inc(g2_done, 1)
                act.wait_ge(var2_done, i + 1)
                nc.scalar.activation(std2[:], mv2[:, :, 1], ACT.Sqrt, bias=epsc[:]).then_inc(std2_done, 1)
                act.wait_ge(t3_ready, i + 1)
                for k, (pa, pb) in enumerate(((m0, m1), (h0, h1))):
                    nc.scalar.copy(tT[:, k, 0:CA], pa[:, 0:CA])
                    last = nc.scalar.copy(tT[:, k, CA:CA + CB], pb[:, 0:CB])
                last.then_inc(tT_done, 1)
                act.wait_ge(top_done, i + 1)
                nc.scalar.activation(ex[:], ex[:], ACT.Exp).then_inc(ex_done, 1)
                act.wait_ge(ct_ready, i + 1)
                nc.scalar.copy(combT[:, 0:CA], m0[0:NX, 0:CA])
                nc.scalar.copy(combT[:, CA:CA + CB], m1[0:NX, 0:CB]).then_inc(ct_done, 1)
                for e in range(NX):
                    if e >= 2:
                        act.wait_ge(y_ready, i * (NX * J) + (e - 1) * J)
                    for f in range(2):
                        act.wait_ge(h_ready, i * (2 * NX) + 2 * e + f + 1)
                        pa, pb = ((m0, m1), (h0, h1))[f]
                        nc.scalar.activation(hT[:, e % 2, f, 0:CA], pa[:, 0:CA], ACT.Gelu, bias=b1[:, e, f:f + 1])
                        nc.scalar.activation(hT[:, e % 2, f, CA:CA + CB], pb[:, 0:CB], ACT.Gelu,
                                             bias=b1[:, e, f:f + 1]).then_inc(h_done, 1)

        @block.vector
        def _(dve):
            step = [0]

            def link(ins):
                step[0] += 1
                ins.then_inc(dve_step, 1)
                dve.wait_ge(dve_step, step[0])

            dve.wait_ge(edges_in, 32)
            link(nc.vector.tensor_scalar(rnd, src, 1.0 / TP, 0.5 / TP - 0.5, ALU.mult, ALU.add))
            link(nc.vector.tensor_scalar(tile_of, rnd, MAGIC, -MAGIC, ALU.add, ALU.add))
            nc.vector.scalar_tensor_tensor(local, tile_of, -float(TP), src, ALU.mult, ALU.add)
            link(nc.vector.tensor_scalar(rnd, dst, 0.5, -0.25, ALU.mult, ALU.add))
            link(nc.vector.tensor_scalar(val1, rnd, MAGIC, -MAGIC, ALU.add, ALU.add))
            link(nc.vector.scalar_tensor_tensor(odd, val1, -2.0, dst, ALU.mult, ALU.add))
            link(nc.vector.tensor_scalar(odd, odd, float(P), 1.0, ALU.mult, ALU.add))
            nc.vector.tensor_tensor(val2, odd, local, ALU.add)
            for t in range(NT):
                if t % J == 0:
                    dve.wait_ge(x_in[t // J], 16)
                last = nc.vector.bn_stats(stats[:, t, :], xb[:, t, :])
            link(last)
            for t in range(NT):
                last = nc.vector.bn_aggr(mv[:, t, :], stats[:, t, :])
            last.then_inc(stats_done, 1)
            for b in range(NT):
                last = nc.vector.tensor_scalar(boh[:, b, :], tile_of, float(b), None, ALU.is_equal)
            link(last)

            dve.wait_ge(std_done, 1)
            link(nc.vector.reciprocal(rstd[:], std[:]))
            nc.vector.scalar_tensor_tensor(shift[:], mv[:, :, 0], -1.0, rstd[:], ALU.mult,
                                           ALU.mult).then_inc(shift_done, 1)

            link(nc.vector.tensor_tensor_scan(flat_cnt, flat_boh, flat_boh, 0.0, ALU.add, ALU.max))
            end = cnt[:, :, EC - 1]
            nc.vector.tensor_copy(edges_of[:, 0:1], end[:, 0:1])
            nc.vector.tensor_tensor(edges_of[:, 1:NT], end[:, 1:NT], end[:, 0:NT - 1],
                                    ALU.subtract).then_inc(counts_ready, 1)
            dve.wait_ge(totals_ready, 1)
            above, total = agg_ps[0:TP, 0:NT], agg_ps[0:TP, NT:2 * NT]
            link(nc.vector.tensor_reduce(fullest[:], total, AX_X, ALU.max))
            nc.vector.tensor_scalar(spill[:], fullest[:], float(BT * P), None, ALU.is_gt).then_inc(spill_known, 1)
            link(nc.vector.tensor_scalar(adj[:], above, -1.0, None, ALU.add))
            link(nc.vector.tensor_tensor(adj[:, 1:NT], adj[:, 1:NT], end[:, 0:NT - 1], ALU.subtract))
            for c0, c1 in ((0, HALF), (HALF, EC)):
                w = c1 - c0
                for b in range(NT):
                    last = nc.vector.scalar_tensor_tensor(prod[:, b, 0:w], cnt[:, b, c0:c1], adj[:, b:b + 1],
                                                          boh[:, b, c0:c1], ALU.add, ALU.mult)
                link(last)
                link(nc.vector.tensor_reduce(pos[:, c0:c1], prod[:, :, 0:w].rearrange("p b c -> p c b"),
                                             AX_X, ALU.add))
            link(nc.vector.tensor_scalar(rnd, pos, 1.0 / P, 0.5 / P - 0.5, ALU.mult, ALU.add))
            link(nc.vector.tensor_scalar(rnd, rnd, MAGIC, -MAGIC, ALU.add, ALU.add))
            nc.vector.scalar_tensor_tensor(place_row, rnd, -float(P), pos, ALU.mult, ALU.add)
            nc.vector.scalar_tensor_tensor(place_col, tile_of, float(BT), rnd, ALU.mult, ALU.add)
            link(nc.vector.tensor_scalar(spilled, pos, float(BT * P), None, ALU.is_ge))
            nc.vector.scalar_tensor_tensor(place_col, spilled, NOWHERE, place_col, ALU.mult, ALU.add)
            link(nc.vector.scalar_tensor_tensor(spill_tile, tile_of, 1.0, spilled, ALU.add, ALU.mult))
            link(nc.vector.tensor_scalar(spill_tile, spill_tile, -1.0, None, ALU.add))

            dve.wait_ge(pool_set, 1)

            def place(n, b):
                dve.wait_ge(oh_used, n + 1)
                dve.sem_inc(passed, 1)
                nc.vector.tensor_tensor(eqh[:, b, :, :], iota_row[:], columns(place_row, n, P),
                                        ALU.is_equal).then_inc(eqh_ready, 1)
                for u in range(PU):
                    last = nc.vector.tensor_scalar(moh[:, b, u, :], iota_col[:], place_col[:, bass.ds(n * PU + u, 1)],
                                                   None, ALU.is_equal)
                last.then_inc(moh_ready, 1)

            with dve.Fori(0, 5) as i:
                for b in range(OB):
                    place(i * OB + b, b)
            dve.wait_ge(zpart0_done, 1)
            nc.vector.tensor_tensor(zrest, z[:], zparts[:, :, 0, :], ALU.subtract).then_inc(zrest_done, 1)
            with dve.Fori(5, 12) as i:
                for b in range(OB):
                    place(i * OB + b, b)
            dve.wait_ge(gnn_in, 64)
            nc.vector.tensor_scalar(z[:], z[:], wself[:, 0:1], None, ALU.mult)
            dve.wait_ge(zpart1_done, 1)
            nc.vector.tensor_tensor(zparts[:, :, 2, :], zrest, zparts[:, :, 1, :],
                                    ALU.subtract).then_inc(zparts_done, 1)
            with dve.Fori(12, BATCHES // OB) as i:
                for b in range(OB):
                    place(i * OB + b, b)
            place(BATCHES - 1, 0)

            dve.wait_ge(placed, 1)
            got1, got2 = h0[:, 0:ST], h1[:, 0:ST]
            link(nc.vector.tensor_scalar(slot_odd[:], got2, float(P), None, ALU.is_ge))
            nc.vector.scalar_tensor_tensor(slot_dst[:], got1, 2.0, slot_odd[:], ALU.mult, ALU.add)
            nc.vector.scalar_tensor_tensor(slot_src[:], slot_odd[:], -float(P), got2, ALU.mult,
                                           ALU.add).then_inc(slots_done, 1)

            with dve.If(dve.value_load(spill[0:1, 0:1], min_val=0, max_val=1) > 0):
                with dve.Fori(0, EC) as c:
                    dve.wait_ge(spill_landed, c * 16 + 16)
                    dve.sem_inc(passed, 1)
                    nc.vector.tensor_scalar(spill_oh, iota_flat[:, 0:TP], local[:, bass.ds(c, 1)], None, ALU.is_equal)
                    nc.vector.tensor_scalar(spill_in, iota_flat[:, 0:NT], spill_tile[:, bass.ds(c, 1)], None,
                                            ALU.is_equal).then_inc(spill_step, 1)
                    dve.wait_ge(spill_step, c + 1)
                    for part in range(3):
                        last = nc.vector.tensor_tensor(
                            spill_rhs[:, part, :, :],
                            spill_rows[:, part, :].rearrange("p (a h) -> p a h", a=1).to_broadcast([TP, NT, H1]),
                            spill_in.rearrange("p (b a) -> p b a", a=1).to_broadcast([TP, NT, H1]), ALU.mult)
                    last.then_inc(spill_ready, 1)
                dve.wait_ge(spill_total, 1)
                for (b0, b1_), ps in zip(SPILL_BANKS, (m0, m1, y0, y1)):
                    last = nc.vector.tensor_tensor(
                        z[:, b0:b1_, :], z[:, b0:b1_, :],
                        ps[0:TP, 0:(b1_ - b0) * H1].rearrange("p (b h) -> p b h", h=H1), ALU.add)
                last.then_inc(spill_added, 1)
                dve.wait_ge(spill_added, 1)
            dve.sem_inc(values_free, 1)

            dve.wait_ge(ctx_ready, 1)
            for c in range(2):
                nc.vector.tensor_tensor(mctx[:, c, :], lg_ps[:, c * P:(c + 1) * P], same_head[:], ALU.mult)
            link(nc.vector.tensor_copy(ksum[:], lg_ps[:, 2 * P:2 * P + 2]))
            for c in range(2):
                last = nc.vector.tensor_scalar(ksb[:, c, :], same_head[:], ksum[:, c:c + 1], None, ALU.mult)
            last.then_inc(ctx_masked, 1)

            def q_whole(t, s):
                dve.wait_ge(eq_done, t + 1)
                dve.wait_ge(qn_done, t + 1)
                nc.vector.scalar_tensor_tensor(qp[:, s, :], (m0, m1)[s][:, 0:CB], 0.0, eq[:, s, :],
                                               ALU.max, ALU.add).then_inc(qp_done, 1)

            def divide(t, s):
                dve.wait_ge(den_ready, t + 3)
                dve.wait_ge(mix_ready, t + 1)
                nc.vector.tensor_scalar(den[:, s, :], (h0, h1)[s][:, 0:CB], 1e-6, None, ALU.max).then_inc(den_read, 1)
                dve.wait_ge(den_read, t + 3)
                nc.vector.reciprocal(den[:, s, :], den[:, s, :]).then_inc(den_inv, 1)
                dve.wait_ge(den_inv, t + 1)
                nc.vector.tensor_tensor(qn[:, s, :], den[:, s, :], qp[:, s, :], ALU.mult).then_inc(qn_done, 1)

            def mix_add(t, s):
                dve.wait_ge(mix_ready, t + 3)
                nc.vector.tensor_tensor(tile(xb, t), tile(xb, t), yslot[s], ALU.add).then_inc(mix_added, 1)

            def q_step(t, s):
                q_whole(t + 1, 1 - s)
                divide(t, s)
                mix_add(t - 1, 1 - s)

            dve.sem_inc(qp_done, 2)
            dve.sem_inc(den_read, 2)
            dve.sem_inc(qn_done, 2)
            dve.sem_inc(mix_added, 2)
            dve.wait_ge(xn_added, NT + 2)
            q_whole(0, 0)
            q_whole(1, 1)
            divide(0, 0)
            with dve.Fori(0, NT // 2 - 1) as i:
                q_step(i * 2 + 1, 1)
                q_step(i * 2 + 2, 0)
            q_step(NT - 2, 1)
            divide(NT - 1, 0)
            mix_add(NT - 2, 1)
            mix_add(NT - 1, 0)

            def node_onehots(g, j):
                dve.wait_ge(bucket_used, g * J + J + max(j - 1, 0))
                dve.sem_inc(passed, 1)
                sources = slot_src[:, bass.ds(g * (J * BT) + j * BT, BT)]
                nc.vector.tensor_tensor(noh[:, j % 2, :, :], iota_node[:],
                                        sources.rearrange("p (a c) -> p a c", a=1).to_broadcast([P, TP, BT]),
                                        ALU.is_equal).then_inc(noh_ready, 1)

            dve.wait_ge(slots_done, 1)
            for j in range(J):
                node_onehots(0, j)

            link0 = step[0]

            def group(i, following):
                n = [0]

                def chain(ins):
                    n[0] += 1
                    ins.then_inc(dve_step, 1)
                    dve.wait_ge(dve_step, i * CHAIN + (link0 + n[0]))

                dve.wait_ge(bucket_used, i * J + 2 * J)
                dve.sem_inc(passed, 1)
                nc.vector.tensor_tensor(hs, z[:, bass.ds(i * J, J), :],
                                        agg_ps[0:TP, 0:J * H1].rearrange("p (j h) -> p j h", j=J),
                                        ALU.add).then_inc(hs_done, 1)
                for j in range(J):
                    dve.wait_ge(g3_ready, i * J + j + 1)
                    h3 = h3slot[j]
                    chain(nc.vector.scalar_tensor_tensor(
                        x2[:, j, :], h3, 0.0, xb[:, bass.ds(i * J + j, 1), :].rearrange("p a d -> p (a d)"),
                        ALU.max, ALU.add))
                    nc.vector.bn_stats(stats2[:, j, :], x2[:, j, :]).then_inc(x2_done, 1)
                dve.wait_ge(x2_done, i * J + J)
                dve.sem_inc(passed, 1)
                for j in range(J):
                    last = nc.vector.bn_aggr(mv2[:, j, :], stats2[:, j, :])
                last.then_inc(var2_done, 1)
                dve.wait_ge(std2_done, i + 1)
                chain(nc.vector.reciprocal(rstd2[:], std2[:]))
                chain(nc.vector.scalar_tensor_tensor(shift2[:], mv2[:, :, 0], -1.0, rstd2[:], ALU.mult, ALU.mult))
                for j in range(J):
                    last = nc.vector.tensor_scalar(tk[:, j, :], x2[:, j, :], rstd2[:, j:j + 1], shift2[:, j:j + 1],
                                                   ALU.mult, ALU.add)
                last.then_inc(tk_done, 1)
                dve.wait_ge(tk_done, i + 1)
                dve.wait_ge(stored, i * 16 + 16)
                chain(nc.vector.tensor_tensor(acc, x2, tk, ALU.add))

                dve.wait_ge(lg_ready, i + 1)
                chain(nc.vector.tensor_copy(lg[:].rearrange("p j x -> p (j x)"), lg_ps[0:TP, 0:J * NX]))
                dve.sem_inc(passed, 1)
                for j in range(J):
                    last = nc.vector.max(top[:, j, :], lg[:, j, :])
                chain(last)
                dve.sem_inc(passed, 1)
                for j in range(J):
                    nc.vector.max_index(top_at[:, j, :], top[:, j, :], lg[:, j, :])
                nc.vector.tensor_tensor(ex[:], top[:], top[:, :, 0:1].to_broadcast([TP, J, NX]),
                                        ALU.subtract).then_inc(top_done, 1)
                dve.wait_ge(top_done, i + 1)
                chain(nc.vector.tensor_copy(top_atf[:], top_at[:]))
                dve.wait_ge(ex_done, i + 1)
                chain(nc.vector.tensor_reduce(exs[:], ex[:], AX_X, ALU.add))
                chain(nc.vector.reciprocal(exs[:], exs[:]))
                chain(nc.vector.tensor_tensor(pw[:], ex[:, :, 0:2],
                                              exs[:].rearrange("p (j a) -> p j a", a=1).to_broadcast([TP, J, 2]),
                                              ALU.mult))
                chain(nc.vector.tensor_tensor(pws[:], pw[:, :, 0], pw[:, :, 1], ALU.add))
                chain(nc.vector.tensor_scalar(pws[:], pws[:], 1e-12, None, ALU.max))
                chain(nc.vector.reciprocal(pws[:], pws[:]))
                chain(nc.vector.tensor_tensor(pw[:], pw[:],
                                              pws[:].rearrange("p (j a) -> p j a", a=1).to_broadcast([TP, J, 2]),
                                              ALU.mult))
                for r2 in range(2):
                    last = nc.vector.tensor_tensor(pick[:, r2, :, :], iota_x[:],
                                                   top_atf[:, :, r2:r2 + 1].to_broadcast([TP, J, NX]), ALU.is_equal)
                chain(last)
                for r2 in range(2):
                    last = nc.vector.tensor_tensor(pick[:, r2, :, :], pick[:, r2, :, :],
                                                   pw[:, :, r2:r2 + 1].to_broadcast([TP, J, NX]), ALU.mult)
                chain(last)
                nc.vector.tensor_tensor(comb[:], pick[:, 0, :, :], pick[:, 1, :, :], ALU.add).then_inc(comb_done, 1)
                for j in range(J):
                    dve.wait_ge(b2_ready, i * J + (2, 2, 4, 4, 5)[j])
                    last = nc.vector.tensor_tensor(acc[:, j, :], acc[:, j, :], b2slot[j], ALU.add).then_inc(acc_set, 1)
                dve.wait_ge(acc_set, (i + 1) * J)
                for e in range(NX):
                    if following is not None and e >= NX - J - 1 and e < NX - 1:
                        node_onehots(following, e - (NX - J - 1))
                    for j in range(J):
                        q = e * J + j
                        dve.wait_ge(y_ready, i * (NX * J) + q + 1)
                        if e > 0:
                            dve.wait_ge(y_read, i * (NX * J) + q - J + 1)
                        nc.vector.scalar_tensor_tensor(acc[:, j, :], yslot[q % 3], comb[:, j, e:e + 1], acc[:, j, :],
                                                       ALU.mult, ALU.add).then_inc(y_read, 1)
                assert n[0] == CHAIN, n[0]

            with dve.Fori(0, G - 1) as i:
                group(i, i + 1)
            group(G - 1, None)

        @block.tensor
        def _(pe):
            def zero(ps, start):
                w = ps.shape[-1]
                return nc.tensor.matmul(ps, zeros[:, 0:ps.shape[0]], zeros[:, 0:w], start=start, stop=not start,
                                        skip_group_check=True)

            pe.sem_inc(oh_used, OB)
            pe.sem_inc(kv_ready, 2)
            pe.sem_inc(ctx_used, 2)
            pe.sem_inc(den_ready, 2)
            pe.sem_inc(mix_ready, 2)
            pe.sem_inc(bucket_used, J)
            pe.sem_inc(spill_summed, 1)
            pe.wait_ge(pool_set, 1)

            nctx = 2 * P + 2
            zero(lg_ps[:, 0:nctx], True)

            def transpose(t, s):
                pe.wait_ge(xn_done, t + 1)
                pe.wait_ge(t1_copied, t + 1)
                for k in range(2):
                    last = nc.tensor.transpose((m0, m1)[s][:, k * TP:(k + 1) * TP],
                                               xn[:, s, k * P:(k + 1) * P], ident[0:TP, 0:TP])
                last.then_inc(t1_ready, 1)

            def z_k_v(t, s):
                pe.wait_ge(t1_copied, t + 3)
                pe.wait_ge(z_copied, t + 1)
                for k in range(2):
                    last = nc.tensor.matmul((h0, h1)[s][0:TP, 0:H1], xnT[:, s, k, :], w1g[:, k, :],
                                            start=(k == 0), stop=(k == 1))
                last.then_inc(z_ready, 1)
                pe.wait_ge(kv_read, t + 1)
                for k in range(2):
                    last = nc.tensor.matmul((y0, y1)[s][0:TP, 0:2 * D], xnT[:, s, k, :], wkv[:, k, :],
                                            start=(k == 0), stop=(k == 1))
                last.then_inc(kv_ready, 1)

            def context(t, s):
                pe.wait_ge(k_done, t + 1)
                for c in range(2):
                    f = slice(c * P, (c + 1) * P)
                    nc.tensor.matmul(lg_ps[:, f], vb[:, s, f], kb[:, s, f], start=False, stop=False,
                                     skip_group_check=True)
                    last = nc.tensor.matmul(lg_ps[:, 2 * P + c:2 * P + c + 1], kb[:, s, f], ones[:, 0:1],
                                            start=False, stop=False, skip_group_check=True)
                last.then_inc(ctx_used, 1)

            def step(t, s):
                transpose(t + 1, 1 - s)
                z_k_v(t, s)
                context(t - 1, 1 - s)

            transpose(0, 0)
            transpose(1, 1)
            pe.wait_ge(gnn_in, 64)
            pe.wait_ge(mix_in, 64)
            z_k_v(0, 0)
            with pe.Fori(0, 2) as i:
                step(i * 2 + 1, 1)
                step(i * 2 + 2, 0)
            pe.wait_ge(counts_ready, 1)
            nc.tensor.matmul(agg_ps[0:TP, 0:NT], before[:], edges_of[:], start=True, stop=True)
            nc.tensor.matmul(agg_ps[0:TP, NT:2 * NT], ones[:], edges_of[:], start=True, stop=True
                             ).then_inc(totals_ready, 1)
            with pe.Fori(2, NT // 2 - 1) as i:
                step(i * 2 + 1, 1)
                step(i * 2 + 2, 0)
            step(NT - 2, 1)
            z_k_v(NT - 1, 0)
            context(NT - 2, 1)
            context(NT - 1, 0)
            zero(lg_ps[:, 0:nctx], False).then_inc(ctx_ready, 1)

            got = (h0[:, 0:ST], h1[:, 0:ST])
            pe.wait_ge(z_copied, NT + 2)
            for v in range(2):
                zero(got[v], True)

            def place(n, b):
                pe.wait_ge(moh_ready, n + 1)
                pe.wait_ge(oh_ready, n + 1)
                pe.wait_ge(oh2_ready, n + 1)
                for u in range(PU):
                    nc.tensor.matmul(got[0], soh1[:, b, u, :], moh[:, b, u, :], start=False, stop=False,
                                     skip_group_check=True)
                    last = nc.tensor.matmul(got[1], soh2[:, b, :, u], moh[:, b, u, :], start=False, stop=False,
                                            skip_group_check=True)
                last.then_inc(oh_used, 1)

            with pe.Fori(0, BATCHES // OB) as i:
                for b in range(OB):
                    place(i * OB + b, b)
            place(BATCHES - 1, 0)
            zero(got[0], False)
            zero(got[1], False).then_inc(placed, 1)

            pe.wait_ge(kv_read, NT + 2)
            pe.wait_ge(spill_known, 1)
            with pe.If(pe.value_load(spill[0:1, 0:1], min_val=0, max_val=1) > 0):
                sums = [(ps[0:TP, 0:(b1_ - b0) * H1], b0, b1_)
                        for (b0, b1_), ps in zip(SPILL_BANKS, (m0, m1, y0, y1))]
                for ps, b0, b1_ in sums:
                    zero(ps, True)
                with pe.Fori(0, EC) as c:
                    pe.wait_ge(spill_ready, c + 1)
                    for part in range(3):
                        for ps, b0, b1_ in sums:
                            last = nc.tensor.matmul(ps, spill_oh,
                                                    spill_rhs[:, part, b0:b1_, :].rearrange("p b h -> p (b h)"),
                                                    start=False, stop=False, skip_group_check=True)
                    last.then_inc(spill_summed, 1)
                for ps, b0, b1_ in sums:
                    last = zero(ps, False)
                last.then_inc(spill_total, 1)
                pe.wait_ge(spill_added, 1)

            pe.wait_ge(ctx_masked, 1)
            for c in range(2):
                nc.tensor.matmul((m0, m1)[c][:, 0:D], mctx[:, c, :], wp[:, c, :], start=True, stop=True
                                 ).then_inc(mout_ready, 1)
            pe.wait_ge(mout_done, 2)

            def queries(t, s):
                pe.wait_ge(qp_done, t + 1)
                for c in range(2):
                    for k in range(2):
                        last = nc.tensor.matmul((m0, m1)[s][:, c * TP:(c + 1) * TP], wq[:, k, c * P:(c + 1) * P],
                                                xnT_all[:, bass.ds(t * (2 * TP) + k * TP, TP)],
                                                start=(k == 0), stop=(k == 1))
                last.then_inc(q_ready, 1)

            def denominators(t, s):
                pe.wait_ge(qp_done, t + 3)
                pe.wait_ge(den_read, t + 1)
                for c in range(2):
                    last = nc.tensor.matmul((h0, h1)[s][:, c * TP:(c + 1) * TP], ksb[:, c, :],
                                            qp[:, s, c * TP:(c + 1) * TP], start=True, stop=True)
                last.then_inc(den_ready, 1)

            def attend(t, s):
                pe.wait_ge(qn_done, t + 3)
                pe.wait_ge(mix_added, t + 1)
                nc.tensor.matmul(yslot[s], ones[0:1, 0:TP], bp[:], start=True, stop=False)
                for c in range(2):
                    last = nc.tensor.matmul(yslot[s], qn[:, s, c * TP:(c + 1) * TP], mout[:, c, :],
                                            start=False, stop=(c == 1))
                last.then_inc(mix_ready, 1)

            def q_step(t, s):
                queries(t + 2, s)
                denominators(t + 1, 1 - s)
                attend(t, s)

            queries(0, 0)
            queries(1, 1)
            denominators(0, 0)
            with pe.Fori(0, NT // 2 - 1) as i:
                q_step(i * 2, 0)
                q_step(i * 2 + 1, 1)
            q_step(NT - 3, 0)
            denominators(NT - 1, 0)
            attend(NT - 2, 1)
            attend(NT - 1, 0)

            def sum_bucket(g, j):
                agg = agg_ps[0:TP, j * H1:(j + 1) * H1]
                pe.wait_ge(landed[j], g * (16 * BT) + 16 * BT)
                pe.wait_ge(noh_ready, g * J + (j + 1))
                for u in range(BT):
                    for part in range(3):
                        last = nc.tensor.matmul(agg, noh[:, j % 2, :, u], rows[:, j * BT + u, part, :],
                                                start=(u == 0 and part == 0), stop=(u == BT - 1 and part == 2))
                last.then_inc(bucket_used, 1)

            for j in range(J):
                sum_bucket(0, j)

            pe.wait_ge(wx_in, 32)
            pe.wait_ge(ffn_in, 48)

            def group(i, following):
                pe.wait_ge(hs_done, i + 1)
                pe.wait_ge(mix_added, NT + 2)
                pe.sem_inc(passed, 1)
                for j in range(J):
                    ps = m0[0:H1, j * TP:(j + 1) * TP] if j < 3 else m1[0:H1, (j - 3) * TP:(j - 2) * TP]
                    last = nc.tensor.transpose(ps, hs[:, j, :], ident[0:TP, 0:TP])
                last.then_inc(g1_ready, 1)
                pe.wait_ge(g1_done, i + 1)
                pe.sem_inc(passed, 1)
                for (lo, hi), ps in zip(SPAN, (h0, h1)):
                    last = nc.tensor.matmul(ps[0:H2, 0:hi - lo], w2g[:], h1T[:, lo:hi], start=True, stop=True)
                last.then_inc(g2_ready, 1)
                pe.wait_ge(g2_done, i + 1)
                for j in range(J):
                    nc.tensor.matmul(h3slot[j], h2T[:, j * TP:(j + 1) * TP], w3g[:],
                                     start=True, stop=True).then_inc(g3_ready, 1)

                pe.wait_ge(tk_done, i + 1)
                for k, (pa, pb) in enumerate(((m0, m1), (h0, h1))):
                    for j in range(J):
                        ps = pa[:, j * TP:(j + 1) * TP] if j < 3 else pb[:, (j - 3) * TP:(j - 2) * TP]
                        last = nc.tensor.transpose(ps, tk[:, j, k * P:(k + 1) * P], ident[0:TP, 0:TP])
                last.then_inc(t3_ready, 1)
                pe.wait_ge(tT_done, i + 1)
                for j in range(J):
                    for k in range(2):
                        last = nc.tensor.matmul(lg_ps[0:TP, j * NX:(j + 1) * NX], tT[:, k, j * TP:(j + 1) * TP],
                                                rw[:, k, :], start=(k == 0), stop=(k == 1))
                last.then_inc(lg_ready, 1)
                pe.wait_ge(comb_done, i + 1)
                for j in range(J):
                    ps = m0[0:NX, j * TP:(j + 1) * TP] if j < 3 else m1[0:NX, (j - 3) * TP:(j - 2) * TP]
                    last = nc.tensor.transpose(ps, comb[:, j, :], ident[0:TP, 0:TP])
                last.then_inc(ct_ready, 1)
                pe.wait_ge(ct_done, i + 1)
                for j in range(J):
                    nc.tensor.matmul(b2slot[j], combT[:, j * TP:(j + 1) * TP], b2[:],
                                     start=True, stop=True).then_inc(b2_ready, 1)

                def first_layer(e):
                    for f in range(2):
                        if e >= 1:
                            pe.wait_ge(h_done, i * (2 * NX) + 2 * (e - 1) + f + 1)
                        for (lo, hi), ps in zip(SPAN, ((m0, m1), (h0, h1))[f]):
                            for k in range(2):
                                last = nc.tensor.matmul(ps[:, 0:hi - lo], w1[:, e, k, f * P:(f + 1) * P],
                                                        tT[:, k, lo:hi], start=(k == 0), stop=(k == 1))
                        last.then_inc(h_ready, 1)

                first_layer(0)
                for e in range(NX):
                    if e + 1 < NX:
                        first_layer(e + 1)
                    if following is not None and e >= NX - J:
                        sum_bucket(following, e - (NX - J))
                    pe.wait_ge(h_done, i * (2 * NX) + 2 * e + 2)
                    for j in range(J):
                        q = e * J + j
                        if q < 3:
                            pe.wait_ge(acc_set, (i + 1) * J)
                        else:
                            pe.wait_ge(y_read, i * (NX * J) + q - 2)
                        for f in range(2):
                            last = nc.tensor.matmul(yslot[q % 3], hT[:, e % 2, f, j * TP:(j + 1) * TP],
                                                    w2[:, e, f, :], start=(f == 0), stop=(f == 1))
                        last.then_inc(y_ready, 1)

            with pe.Fori(0, G - 1) as i:
                group(i, i + 1)
            group(G - 1, None)


CHAIN = 20


def kernel(**inputs):
    import numpy as np
    import concourse.bacc as bacc
    from concourse.bass_utils import run_bass_kernel_spmd

    g = {k: np.asarray(v) for k, v in inputs.items()}
    arrays = {
        "x": g["x"], "src": g["src"], "dst": g["dst"], "w": g["L0_gnn_w"],
        "W1T": g["L0_gnn_W1"].T, "W2T": g["L0_gnn_W2"].T, "W3T": g["L0_gnn_W3"].T,
        "WqT": g["L0_mix_Wq"].T, "WkvT": g["L0_mix_Wkv"].T, "WpT": g["L0_mix_Wproj"].T,
        "bp": g["L0_mix_bproj"], "rT": g["L0_ffn_router_w"].T,
        "w1": g["L0_ffn_w1"], "w2": g["L0_ffn_w2"], "b2": g["L0_ffn_b2"],
        "b1T": g["L0_ffn_b1"].reshape(NX * 2, P).T,
    }
    arrays = {k: np.ascontiguousarray(v) for k, v in arrays.items()}
    nc = bacc.Bacc("TRN2", target_bir_lowering=False, num_devices=1)
    a = {k: nc.dram_tensor(f"in_{k}", v.shape, mybir.dt.from_np(v.dtype), kind="ExternalInput").ap()
         for k, v in arrays.items()}
    out = nc.dram_tensor("out", (N, D), F32, kind="ExternalOutput").ap()
    build(nc, a, out)
    r = run_bass_kernel_spmd(nc, [{f"in_{k}": v for k, v in arrays.items()}], core_ids=[0])
    return r.results[0]["out"]
```

```python
from contextlib import ExitStack

import concourse.bass as bass
import concourse.mybir as mybir
from concourse.alu_op_type import AluOpType as ALU

F32, F16, BF16 = mybir.dt.float32, mybir.dt.float16, mybir.dt.bfloat16
F32R = mybir.dt.float32r
I32, U32 = mybir.dt.int32, mybir.dt.uint32
ACT = mybir.ActivationFunctionType
AX_X = mybir.AxisListType.X

N, D = 3125, 256
NE = 53125
TP = 125
NT = N // TP
J = 5
G = NT // J
EC = NE // TP
P = 128
BT = 18
ST = NT * BT
H1, H2 = 64, 32
NX = 8
HD = 32
NH = D // HD
EPS = 1e-5
PU = 5
BATCHES = EC // PU
OB = 4
HALF = (EC + 1) // 2
MAGIC = 12582912.0
CA, CB = 3 * TP, 2 * TP
SPAN = [(0, CA), (CA, CA + CB)]
ATTEND_AHEAD = [(2, (0, 5)), (3, (5, 9)), (None, (9, NT // 2 - 1))]
WR = J * TP + 1
SPAN_R = [(0, 314), (314, WR)]
NK = 5
NEW = 4
NOWHERE = 600.0
SPILL_BANKS = [(0, 7), (7, 13), (13, 19), (19, 25)]
assert EC % PU == 0 and BATCHES % OB == 1 and NT % 2 == 1 and NK % 2 == 1 and ST <= 512


def build(nc, a, out):
    ztab = nc.dram_tensor("ztab", (N, 3 * H1), BF16, kind="Internal").ap()
    with ExitStack() as ctx:
        def sb(name, shape, dt=F32):
            return ctx.enter_context(nc.sbuf_tensor(name, shape, dt))

        def sem(name):
            return ctx.enter_context(nc.semaphore(name))

        bank = [ctx.enter_context(nc.psum_tensor(f"bank{i}", [P, 512], F32)) for i in range(8)]
        m0, m1, h0, h1, y0, y1, agg_ps, lg_ps = bank
        yslot = [b[0:TP, 0:D] for b in (y0, y1)]
        hbank = (m0, m1, h0)
        c0, c1 = h1, lg_ps
        part_sums = (agg_ps, c1)
        by_token = [c0[0:TP, 0:D], c0[0:TP, D:2 * D], c1[0:TP, 0:D], c1[0:TP, D:2 * D], c0[0:TP, 0:D]]

        xb = sb("xb", [TP, NT, D])
        z = sb("z", [TP, NT, H1])

        class Region:

            def __init__(self, name, words):
                with nc.sbuf_tensor(name, [P, words], F32) as first:
                    self.t, self.at, self.words = first, 0, words
                self.rounded = sb(name + "_r", [P, words], F32R)

            def restart(self):
                self.at = 0
                return self

            def take_rounded(self, rows, n):
                self.at += n
                assert self.at <= self.words
                return self.rounded[0:rows, self.at - n:self.at]

            def take(self, rows, n, dt=F32):
                words = n if dt in (F32, I32) else (n + 1) // 2
                v = self.t[0:rows, self.at:self.at + words]
                self.at += words
                assert self.at <= self.words
                return v if dt == F32 else v.bitcast(dt)[:, 0:n]

        r = Region("region_xn", NT * D)
        xnT_all = r.take(P, NT * 2 * TP)
        r.restart()
        t_hi = r.take_rounded(P, 2 * WR).rearrange("p (k n) -> p k n", k=2)
        t_lo = r.take_rounded(P, 2 * WR).rearrange("p (k n) -> p k n", k=2)
        hT = r.take(P, 4 * J * TP).rearrange("p (s f n) -> p s f n", s=2, f=2)
        h1T = r.take(H1, J * TP)
        h2T = r.take(H2, J * TP)
        combT = h1T[0:NX, :]
        lgT = h2T[0:NX, :]

        r = Region("region_buckets", NT * EC + 1)
        flat_boh = r.take(TP, NT * EC, F16)
        flat_cnt = r.take(TP, NT * EC, F16)
        boh = flat_boh.rearrange("p (b c) -> p b c", b=NT)
        cnt = flat_cnt.rearrange("p (b c) -> p b c", b=NT)
        r.restart()
        moh = r.take(TP, OB * PU * ST, F16).rearrange("p (b u n) -> p b u n", b=OB, u=PU)
        eqh = r.take(TP, OB * P * PU, F16).rearrange("p (b n u) -> p b n u", b=OB, u=PU)
        soh1 = r.take(TP, OB * P * PU, F16).rearrange("p (b u n) -> p b u n", b=OB, u=PU)
        soh2 = r.take(TP, OB * P * PU, F16).rearrange("p (b n u) -> p b n u", b=OB, u=PU)
        r.restart()
        x2 = r.take(TP, J * D).rearrange("p (j d) -> p j d", j=J)
        tk = r.take(TP, J * D).rearrange("p (j d) -> p j d", j=J)
        acc = r.take(TP, J * D).rearrange("p (j d) -> p j d", j=J)
        late = r.at
        kb2 = r.take(TP, 2 * D).rearrange("p (s d) -> p s d", s=2)
        vb2 = r.take(TP, 2 * D).rearrange("p (s d) -> p s d", s=2)
        ek2 = r.take(TP, 2 * D).rearrange("p (s d) -> p s d", s=2)
        r.at = late
        eq = r.take(P, 4 * TP).rearrange("p (s n) -> p s n", s=2)
        qp = r.take(P, 4 * TP).rearrange("p (s n) -> p s n", s=2)
        den = r.take(P, 4 * TP)
        mctx = den[:, 0:2 * P].rearrange("p (c n) -> p c n", c=2)
        den = den[0:TP, 0:4 * NH].rearrange("p (v s n) -> p v s n", v=2, s=2)
        qn = r.take(P, 4 * TP).rearrange("p (s n) -> p s n", s=2)
        hs = r.take(TP, J * H1).rearrange("p (j h) -> p j h", j=J)
        wide = acc[:, 0:2, :]
        w1_hi_b = r.take_rounded(P, (NX - NEW) * 2 * D).rearrange("p (e k f) -> p e k f", e=NX - NEW, k=2)
        noh = r.take(P, 2 * TP * BT, BF16).rearrange("p (s n c) -> p s n c", s=2, c=BT)

        r = Region("region_rows", J * BT * 3 * H1 // 2)
        prod = r.take(TP, NT * HALF).rearrange("p (b c) -> p b c", b=NT)
        xn = r.take(TP, 2 * D).rearrange("p (s d) -> p s d", s=2)
        kb = r.take(TP, 2 * D).rearrange("p (s d) -> p s d", s=2)
        vb = r.take(TP, 2 * D).rearrange("p (s d) -> p s d", s=2)
        ek = r.take(TP, 2 * D).rearrange("p (s d) -> p s d", s=2)
        r.restart()
        spill_rows = r.take(TP, 3 * H1, BF16).rearrange("p (s h) -> p s h", s=3)
        spill_rhs = r.take(TP, 3 * NT * H1, BF16).rearrange("p (s b h) -> p s b h", s=3, b=NT)
        spill_oh = r.take(TP, TP, BF16)
        spill_in = r.take(TP, NT, BF16)
        spill_dst = r.take(TP, 1, I32)
        r.restart()
        rows = r.take(P, J * BT * 3 * H1, BF16).rearrange("p (r s h) -> p r s h", r=J * BT, s=3)

        r = Region("region_w1", NX * 2 * D)
        zparts = r.take(TP, NT * 3 * H1, BF16).rearrange("p (t s h) -> p t s h", t=NT, s=3)
        zrest = r.take(TP, NT * H1).rearrange("p (t h) -> p t h", t=NT)
        r.restart()
        w1 = r.take(P, NX * 2 * D).rearrange("p (e k f) -> p e k f", e=NX, k=2)

        r.restart()
        w1_lo = r.take_rounded(P, NX * 2 * D).rearrange("p (e k f) -> p e k f", e=NX, k=2)

        r = Region("region_w2", NX * 2 * D)
        src = r.take(TP, EC, I32)
        dst = r.take(TP, EC, I32)
        rnd = r.take(TP, EC)
        tile_of = r.take(TP, EC, F16)
        local = r.take(TP, EC)
        val1 = r.take(TP, EC)
        odd = r.take(TP, EC)
        val2 = r.take(TP, EC, F16)
        pos = r.take(TP, EC)
        place_row = r.take(TP, EC, F16)
        spilled = r.take(TP, EC)
        place_col = odd
        spill_tile = pos
        r.restart()
        w2 = r.take(P, NX * 2 * D).rearrange("p (e k f) -> p e k f", e=NX, k=2)

        w1_hi_a = sb("w1_hi_a", [P, NEW, 2, D], F32R)
        rw_hi = sb("rw_hi", [P, 2, NX], F32R)
        rw_lo = sb("rw_lo", [P, 2, NX], F32R)
        xnT = sb("xnT", [P, 2, 2, TP])

        wq = sb("wq", [P, 2, D])
        wkv = sb("wkv", [P, 2, 2 * D])
        wp = sb("wp", [P, 2, D])
        w1g = sb("w1g", [P, 2, H1])
        w2g = sb("w2g", [H1, H2])
        w3g = sb("w3g", [H2, D])
        rw = sb("rw", [P, 2, NX])
        b1 = sb("b1", [P, NX, 2])
        b2 = sb("b2", [NX, D])
        bp = sb("bp", [TP, D])
        wself = sb("wself", [TP, 1])

        ident = sb("ident", [P, P])
        before = sb("before", [TP, TP])
        ones = sb("ones", [TP, TP])
        same_head = sb("same_head", [P, P])
        zeros = sb("zeros", [P, 512], BF16)
        iota_col = sb("iota_col", [TP, ST], F16)
        iota_row = sb("iota_row", [TP, P, PU], F16)
        iota_flat = sb("iota_flat", [TP, P], F16)
        iota_node = sb("iota_node", [P, TP, BT], BF16)
        iota_x = sb("iota_x", [TP, J, NX])
        epsc = sb("epsc", [TP, 1])

        stats = sb("stats", [TP, NT, 6])
        mv = sb("mv", [TP, NT, 2])
        std = sb("std", [TP, NT])
        rstd = sb("rstd", [TP, NT])
        shift = sb("shift", [TP, NT])

        edges_of = sb("edges_of", [TP, NT])
        adj = sb("adj", [TP, NT])
        fullest = sb("fullest", [TP, 1])
        spill = sb("spill", [TP, 1], I32)
        slot_odd = sb("slot_odd", [P, ST])
        slot_dst = sb("slot_dst", [P, ST], I32)
        slot_src = sb("slot_src", [P, ST], BF16)
        now_dst = sb("now_dst", [P, J * BT], I32)

        mout = sb("mout", [P, 2, D])
        ksum = sb("ksum", [P, 2])
        ksum_of = sb("ksum_of", [P, 2, NH])

        stats2 = sb("stats2", [TP, J, 6])
        mv2 = sb("mv2", [TP, J, 2])
        std2 = sb("std2", [TP, J])
        rstd2 = sb("rstd2", [TP, J])
        shift2 = sb("shift2", [TP, J])
        lg = sb("lg", [TP, J, NX])
        top = sb("top", [TP, J, NX])
        top_at = sb("top_at", [TP, J, NX], U32)
        top_atf = sb("top_atf", [TP, J, NX])
        ex = sb("ex", [TP, J, NX])
        exs = sb("exs", [TP, J])
        pw = sb("pw", [TP, J, 2])
        pws = sb("pws", [TP, J])
        pick = sb("pick", [TP, 2, J, NX])
        comb = sb("comb", [TP, J, NX])

        edges_in, gnn_in, mix_in, ffn_in, w2_in = map(sem, ("edges_in", "gnn_in", "mix_in", "ffn_in", "w2_in"))
        x_in = [sem(f"x_in{g}") for g in range(G)]
        pool_set, pool_step, dve_step, act_step = map(sem, ("pool_set", "pool_step", "dve_step", "act_step"))
        stats_done, std_done, shift_done, xn_done = map(sem, ("stats_done", "std_done", "shift_done", "xn_done"))
        t1_ready, t1_copied, z_ready, z_copied = map(sem, ("t1_ready", "t1_copied", "z_ready", "z_copied"))
        zpart0_done, zrest_done, zpart1_done, zparts_done, ztab_stored = map(sem, (
            "zpart0_done", "zrest_done", "zpart1_done", "zparts_done", "ztab_stored"))
        counts_ready, totals_ready, eqh_ready, moh_ready, oh_ready, oh2_ready, oh_used, placed, slots_done = map(sem, (
            "counts_ready", "totals_ready", "eqh_ready", "moh_ready", "oh_ready", "oh2_ready", "oh_used", "placed",
            "slots_done"))
        spill_known, spill_landed, spill_ready, spill_summed, spill_total, spill_added, values_free = map(sem, (
            "spill_known", "spill_landed", "spill_ready", "spill_summed", "spill_total", "spill_added",
            "values_free"))
        spill_step, stats2_done, drained, bp_added, den_spread, widened = map(sem, (
            "spill_step", "stats2_done", "drained", "bp_added", "den_spread", "widened"))
        w1_in, w1_hi_done, w1_lo_done, t_hi_done, t_lo_done, lgT_ready, lgT_done, pad_set = map(sem, (
            "w1_in", "w1_hi_done", "w1_lo_done", "t_hi_done", "t_lo_done", "lgT_ready", "lgT_done", "pad_set"))
        xnT_kept, xnT_back, xn_added, kv_ready, kv_read, ek_done, k_done, ctx_used = map(sem, (
            "xnT_kept", "xnT_back", "xn_added", "kv_ready", "kv_read", "ek_done", "k_done", "ctx_used"))
        ctx_ready, ctx_masked, mout_ready, mout_done = map(sem, (
            "ctx_ready", "ctx_masked", "mout_ready", "mout_done"))
        q_ready, eq_done, qp_done, den_ready, den_read, den_inv, qn_done, mix_ready, mix_added = map(sem, (
            "q_ready", "eq_done", "qp_done", "den_ready", "den_read", "den_inv", "qn_done", "mix_ready",
            "mix_added"))
        landed = [sem(f"landed{j}") for j in range(J)]
        noh_ready, bucket_used = map(sem, ("noh_ready", "bucket_used"))
        hs_done, g1_ready, g1_done, g2_ready, g2_done, g3_ready, x2_done = map(sem, (
            "hs_done", "g1_ready", "g1_done", "g2_ready", "g2_done", "g3_ready", "x2_done"))
        var2_done, std2_done, tk_done, t3_ready = map(sem, (
            "var2_done", "std2_done", "tk_done", "t3_ready"))
        lg_ready, top_done, ex_done, comb_done, ct_ready, ct_done, b2_ready, acc_set = map(sem, (
            "lg_ready", "top_done", "ex_done", "comb_done", "ct_ready", "ct_done", "b2_ready", "acc_set"))
        h_ready, h_done, y_ready, y_read, stored = map(sem, ("h_ready", "h_done", "y_ready", "y_read", "stored"))

        dst_copied = sem("dst_copied")
        kv_in, eps_set, iotas_set = map(sem, ("kv_in", "eps_set", "iotas_set"))
        passed = sem("passed")

        def tile(x, t):
            return x[:, bass.ds(t, 1), :].rearrange("p a d -> p (a d)")

        def columns(v, n, w):
            return v[:, bass.ds(n * PU, PU)].rearrange("p (a u) -> p a u", a=1).to_broadcast([TP, w, PU])

        def w1_hi(e):
            return w1_hi_a[:, e, :, :] if e < NEW else w1_hi_b[:, e - NEW, :, :]

        block = ctx.enter_context(nc.Block())

        @block.sync
        def _(sp):
            sp.sem_inc(stored, 16)
            def load_x(g):
                sp.dma_start(xb[:, g * J:(g + 1) * J, :],
                             a["x"].rearrange("(g t p) d -> g p t d", p=TP, g=G)[g]).then_inc(x_in[g], 16)

            load_x(0)
            sp.dma_start(src, a["src"].rearrange("(p c) -> p c", p=TP)).then_inc(edges_in, 16)
            sp.dma_start(dst, a["dst"].rearrange("(p c) -> p c", p=TP)).then_inc(edges_in, 16)
            load_x(1)
            sp.dma_start(w1g[:], a["W1T"].rearrange("(k p) h -> p k h", p=P)).then_inc(gnn_in, 16)
            sp.dma_start(wself[:], a["w"].rearrange("(a b) -> a b", a=1).to_broadcast([TP, 1])).then_inc(gnn_in, 16)
            sp.dma_start(w2g[:], a["W2T"]).then_inc(gnn_in, 16)
            sp.dma_start(w3g[:], a["W3T"]).then_inc(gnn_in, 16)
            sp.dma_start(wkv[:], a["WkvT"].rearrange("(k p) h -> p k h", p=P)).then_inc(kv_in, 16)
            for g in range(2, G):
                load_x(g)
            sp.dma_start(wq[:], a["WqT"].rearrange("(k p) h -> p k h", p=P)).then_inc(mix_in, 16)
            sp.dma_start(wp[:], a["WpT"].rearrange("(k p) h -> p k h", p=P)).then_inc(mix_in, 16)
            sp.dma_start(bp[:], a["bp"].rearrange("(a d) -> a d", a=1).to_broadcast([TP, D])).then_inc(mix_in, 16)
            sp.dma_start(rw[:], a["rT"].rearrange("(k p) h -> p k h", p=P)).then_inc(ffn_in, 16)
            sp.dma_start(b1[:], a["b1T"].rearrange("p (e k) -> p e k", e=NX)).then_inc(ffn_in, 16)
            sp.dma_start(b2[:], a["b2"]).then_inc(ffn_in, 16)
            sp.wait_ge(zparts_done, 1)
            sp.dma_start(ztab.rearrange("(t p) h -> p t h", p=TP),
                         zparts.rearrange("p t s h -> p t (s h)")).then_inc(ztab_stored, 16)
            sp.wait_ge(ztab_stored, 16)
            sp.dma_start(w1, a["w1"].rearrange("e (k p) f -> p e k f", p=P)).then_inc(w1_in, 16)
            sp.wait_ge(values_free, 1)
            sp.dma_start(w2, a["w2"].rearrange("e (k p) f -> p e k f", p=P)).then_inc(w2_in, 16)
            with sp.Fori(0, G) as i:
                sp.wait_ge(y_read, (i + 1) * NX * J + 2)
                sp.dma_start(out.rearrange("(g j p) d -> g p j d", p=TP, j=J)[bass.ds(i, 1), :, :, :]
                             .rearrange("g p j d -> p (g j) d"), acc).then_inc(stored, 16)
                sp.wait_ge(stored, (i + 2) * 16)
                sp.sem_inc(passed, 1)

        @block.gpsimd
        def _(pool):
            nc.gpsimd.memset(epsc[:], EPS).then_inc(eps_set, 1)
            nc.gpsimd.memset(ident[:], 0.0).then_inc(pool_step, 1)
            nc.gpsimd.memset(before[:], 1.0).then_inc(pool_step, 1)
            nc.gpsimd.memset(same_head[:], 1.0).then_inc(pool_step, 1)
            nc.gpsimd.memset(ones[:], 1.0)
            nc.gpsimd.memset(zeros[:], 0.0)
            pool.wait_ge(pool_step, 3)
            nc.gpsimd.affine_select(out=ident[:], in_=ident[:], compare_op=ALU.not_equal, fill=1.0, base=0,
                                    pattern=[[-1, P]], channel_multiplier=1)
            nc.gpsimd.affine_select(out=before[:], in_=before[:], compare_op=ALU.is_gt, fill=0.0, base=0,
                                    pattern=[[1, TP]], channel_multiplier=-1)
            blocks = same_head[:].rearrange("p (b c) -> p b c", c=HD)
            nc.gpsimd.affine_select(out=blocks, in_=blocks, compare_op=ALU.is_ge, fill=0.0, base=0,
                                    pattern=[[-HD, P // HD], [0, HD]], channel_multiplier=1).then_inc(pool_step, 1)
            pool.wait_ge(pool_step, 4)
            nc.gpsimd.affine_select(out=blocks, in_=blocks, compare_op=ALU.is_ge, fill=0.0, base=HD - 1,
                                    pattern=[[HD, P // HD], [0, HD]], channel_multiplier=-1).then_inc(pool_set, 1)

            nc.gpsimd.iota(iota_col[:], [[1, ST]], base=0, channel_multiplier=0,
                           allow_small_or_imprecise_dtypes=True)
            nc.gpsimd.iota(iota_row[:], [[1, P], [0, PU]], base=0, channel_multiplier=0,
                           allow_small_or_imprecise_dtypes=True)
            nc.gpsimd.iota(iota_flat[:], [[1, P]], base=0, channel_multiplier=0,
                           allow_small_or_imprecise_dtypes=True)
            nc.gpsimd.iota(iota_node[:], [[1, TP], [0, BT]], base=1, channel_multiplier=0,
                           allow_small_or_imprecise_dtypes=True)
            nc.gpsimd.iota(iota_x[:], [[0, J], [1, NX]], base=0, channel_multiplier=0,
                           allow_small_or_imprecise_dtypes=True).then_inc(iotas_set, 1)

            pool.sem_inc(xn_added, 2)
            pool.sem_inc(xnT_kept, 2)

            def keep(t, s):
                pool.wait_ge(xn_done, t + 1)
                pool.sem_inc(passed, 1)
                nc.gpsimd.tensor_tensor(tile(xb, t), tile(xb, t), xn[:, s, :], ALU.add).then_inc(xn_added, 1)
                pool.wait_ge(t1_copied, t + 3)
                nc.gpsimd.tensor_copy(xnT_all[:, bass.ds(t * (2 * TP), 2 * TP)],
                                      xnT[:, s, :, :].rearrange("p k n -> p (k n)")).then_inc(xnT_kept, 1)

            def add_halves(t, s):
                pool.wait_ge(ek_done, t + 1)
                nc.gpsimd.tensor_tensor(kb[:, s, :], kb[:, s, :], ek[:, s, :], ALU.add).then_inc(k_done, 1)

            with pool.Fori(0, NK // 2) as i:
                for s in range(2):
                    keep(i * 2 + s, s)
                    add_halves(i * 2 + s, s)
            keep(NK - 1, 0)
            add_halves(NK - 1, 0)
            with pool.Fori(NK // 2, NT // 2) as i:
                keep(i * 2 + 1, 1)
                keep(i * 2 + 2, 0)

            def second_value(n, b):
                pool.wait_ge(eqh_ready, n + 1)
                pool.sem_inc(passed, 1)
                nc.gpsimd.tensor_tensor(soh2[:, b, :, :], eqh[:, b, :, :], columns(val2, n, P), ALU.mult
                                        ).then_inc(oh2_ready, 1)

            pool.wait_ge(mix_in, 48)
            for g in range(G):
                with pool.Fori(g * 4, g * 4 + 4) as i:
                    for b in range(OB):
                        second_value(i * OB + b, b)
                here = xb[:, g * J:(g + 1) * J, :]
                pool.wait_ge(xn_added, NT + 2)
                nc.gpsimd.tensor_tensor(here, here, bp[:].rearrange("p (a d) -> p a d", a=1).to_broadcast([TP, J, D]),
                                        ALU.add).then_inc(bp_added, 1)
            with pool.Fori(G * 4, BATCHES // OB) as i:
                for b in range(OB):
                    second_value(i * OB + b, b)
            second_value(BATCHES - 1, 0)

            pool.wait_ge(ztab_stored, 16)
            pool.wait_ge(spill_known, 1)
            with pool.If(pool.value_load(spill[0:1, 0:1], min_val=0, max_val=1) > 0):
                with pool.Fori(0, EC) as c:
                    pool.wait_ge(spill_summed, c + 1)
                    nc.gpsimd.tensor_copy(spill_dst, dst[:, bass.ds(c, 1)]).then_inc(pool_step, 1)
                    pool.wait_ge(pool_step, c + 5)
                    pool.sem_inc(passed, 1)
                    nc.gpsimd.indirect_dma_start(
                        spill_rows.rearrange("p s h -> p (s h)"), None, ztab,
                        bass.IndirectOffsetOnAxis(spill_dst, 0)).then_inc(spill_landed, 16)
                pool.wait_ge(spill_added, 1)

            pool.wait_ge(slots_done, 1)
            with pool.Fori(0, G) as i:
                for j in range(J):
                    pool.wait_ge(bucket_used, i * J + (j + 1))
                    here = slice(j * BT, (j + 1) * BT)
                    nc.gpsimd.tensor_copy(now_dst[:, here],
                                          slot_dst[:, bass.ds(i * (J * BT) + j * BT, BT)]).then_inc(dst_copied, 1)
                    pool.wait_ge(dst_copied, i * J + (j + 1))
                    pool.sem_inc(passed, 1)
                    for u in range(j * BT, (j + 1) * BT):
                        nc.gpsimd.indirect_dma_start(
                            rows[:, u, :, :].rearrange("p s h -> p (s h)"), None, ztab,
                            bass.IndirectOffsetOnAxis(now_dst[:, u:u + 1], 0)).then_inc(landed[j], 16)
            for j in range(J):
                pool.wait_ge(landed[j], 16 * BT * G)

        @block.scalar
        def _(act):
            act.wait_ge(eps_set, 1)
            act.wait_ge(stats_done, 1)
            nc.scalar.activation(std[:, 0:J], mv[:, 0:J, 1], ACT.Sqrt, bias=epsc[:]).then_inc(std_done, 1)
            act.wait_ge(shift_done, 1)

            def normalize(t, s):
                act.wait_ge(xn_added, t + 1)
                nc.scalar.activation(xn[:, s, :], tile(xb, t), ACT.Identity, scale=rstd[:, bass.ds(t, 1)],
                                     bias=shift[:, bass.ds(t, 1)]).then_inc(xn_done, 1)

            def copy_transposed(t, s, with_k=True):
                act.wait_ge(t1_ready, t + 1)
                act.wait_ge(kv_ready, t + 1 if with_k else NK + 2)
                act.wait_ge(xnT_kept, t + 1)
                nc.scalar.copy(xnT[:, s, :, :], (m0, m1)[s][:, 0:CB].rearrange("p (k n) -> p k n", k=2)
                               ).then_inc(t1_copied, 1)

            def copy_z(t, s):
                act.wait_ge(z_ready, t + 1)
                nc.scalar.copy(tile(z, t), (h0, h1)[s][0:TP, 0:H1]).then_inc(z_copied, 1)

            def k_and_v(t, s):
                kv = (y0, y1)[s]
                act.wait_ge(kv_ready, t + 3)
                act.wait_ge(ctx_used, t + 1)
                nc.scalar.activation(ek[:, s, :], kv[0:TP, 0:D], ACT.Relu, scale=-1.0).then_inc(act_step, 1)
                nc.scalar.activation(kb[:, s, :], kv[0:TP, 0:D], ACT.Relu)
                nc.scalar.copy(vb[:, s, :], kv[0:TP, D:2 * D]).then_inc(kv_read, 1)
                act.wait_ge(act_step, t + 1)
                nc.scalar.activation(ek[:, s, :], ek[:, s, :], ACT.Exp, scale=-1.0).then_inc(ek_done, 1)

            act.sem_inc(t1_copied, 2)
            act.sem_inc(z_copied, 2)
            act.sem_inc(kv_read, 2)
            normalize(0, 0)
            normalize(1, 1)
            copy_transposed(0, 0)

            def step(t, s, with_k=True):
                copy_transposed(t + 1, 1 - s, with_k)
                normalize(t + 2, s)
                copy_z(t, s)
                if with_k:
                    k_and_v(t, s)

            step(0, 0)
            act.wait_ge(stats_done, 2)
            nc.scalar.activation(std[:, J:NT], mv[:, J:NT, 1], ACT.Sqrt, bias=epsc[:]).then_inc(std_done, 1)
            act.wait_ge(shift_done, 2)
            with act.Fori(0, NK // 2) as i:
                step(i * 2 + 1, 1)
                step(i * 2 + 2, 0)
            with act.Fori(NK // 2, NT // 2 - 1) as i:
                step(i * 2 + 1, 1, False)
                step(i * 2 + 2, 0, False)
            copy_transposed(NT - 1, 0, False)
            copy_z(NT - 2, 1)
            copy_z(NT - 1, 0)

            act.wait_ge(z_copied, NT + 2)
            nc.scalar.copy(zparts[:, :, 0, :], z[:]).then_inc(zpart0_done, 1)

            def first_value(n, b):
                act.wait_ge(eqh_ready, n + 1)
                for u in range(PU):
                    last = nc.scalar.activation(soh1[:, b, u, :], eqh[:, b, :, u], ACT.Copy,
                                                scale=val1[:, bass.ds(n * PU + u, 1)])
                last.then_inc(oh_ready, 1)

            with act.Fori(0, BATCHES // OB // 2) as i:
                for b in range(OB):
                    first_value(i * OB + b, b)
            act.wait_ge(zrest_done, 1)
            nc.scalar.copy(zparts[:, :, 1, :], zrest).then_inc(zpart1_done, 1)
            with act.Fori(BATCHES // OB // 2, BATCHES // OB) as i:
                for b in range(OB):
                    first_value(i * OB + b, b)
            first_value(BATCHES - 1, 0)

            act.wait_ge(placed, 1)

            def bring(t, s):
                act.wait_ge(kv_ready, t + 1)
                act.sem_inc(passed, 1)
                nc.scalar.copy(xnT[:, s, :, :].rearrange("p k n -> p (k n)"),
                               xnT_all[:, bass.ds(t * (2 * TP), 2 * TP)]).then_inc(xnT_back, 1)

            def late_k_and_v(t, s):
                kv = (y0, y1)[s]
                act.wait_ge(kv_ready, t + 3)
                act.wait_ge(ctx_used, t + 1)
                nc.scalar.activation(ek2[:, s, :], kv[0:TP, 0:D], ACT.Relu, scale=-1.0).then_inc(act_step, 1)
                nc.scalar.copy(vb2[:, s, :], kv[0:TP, D:2 * D])
                act.wait_ge(act_step, t + 1)
                nc.scalar.activation(ek2[:, s, :], ek2[:, s, :], ACT.Exp, scale=-1.0).then_inc(ek_done, 1)

            act.wait_ge(xnT_kept, NT + 2)
            bring(NK, 1)
            with act.Fori(NK // 2, NT // 2 - 1) as i:
                bring(i * 2 + 2, 0)
                late_k_and_v(i * 2 + 1, 1)
                bring(i * 2 + 3, 1)
                late_k_and_v(i * 2 + 2, 0)
            bring(NT - 1, 0)
            late_k_and_v(NT - 2, 1)
            late_k_and_v(NT - 1, 0)

            act.wait_ge(w1_in, 16)
            act.wait_ge(ffn_in, 48)
            nc.scalar.copy(rw_hi[:], rw[:]).then_inc(w1_hi_done, 1)
            for e in range(NX):
                nc.scalar.copy(w1_hi(e), w1[:, e, :, :]).then_inc(w1_hi_done, 1)

            for c in range(2):
                act.wait_ge(mout_ready, c + 1)
                nc.scalar.copy(mout[:, c, :], (m0, m1)[c][:, 0:D]).then_inc(mout_done, 1)

            def q_half(t, s):
                act.wait_ge(q_ready, t + 1)
                act.wait_ge(qp_done, t + 1)
                nc.scalar.activation(eq[:, s, :], (m0, m1)[s][:, 0:CB], ACT.Relu, scale=-1.0).then_inc(act_step, 1)
                act.wait_ge(act_step, t + (NT + 1))
                nc.scalar.activation(eq[:, s, :], eq[:, s, :], ACT.Exp, scale=-1.0).then_inc(eq_done, 1)

            def widen(t, s):
                act.wait_ge(den_inv, t + 1)
                act.wait_ge(den_spread, t + 1)
                nc.scalar.copy(wide[:, s, :].rearrange("p (h a) -> p h a", a=HD),
                               den[:, 1, s, :].rearrange("p (h a) -> p h a", a=1).to_broadcast([TP, NH, HD])
                               ).then_inc(widened, 1)

            q_half(0, 0)
            q_half(1, 1)
            widen(0, 0)
            q_half(2, 0)
            widen(1, 1)
            with act.Fori(0, NT // 2 - 1) as i:
                widen(i * 2 + 2, 0)
                q_half(i * 2 + 3, 1)
                widen(i * 2 + 3, 1)
                q_half(i * 2 + 4, 0)
            widen(NT - 1, 0)

            def relu_g1(g):
                act.wait_ge(g1_ready, g + 1)
                nc.scalar.activation(h1T[:, 0:CA], c0[0:H1, 0:CA], ACT.Relu)
                nc.scalar.activation(h1T[:, CA:CA + CB], c1[0:H1, 0:CB], ACT.Relu).then_inc(g1_done, 1)

            def relu_g2(g):
                act.wait_ge(g2_ready, g + 1)
                nc.scalar.activation(h2T[:, 0:CA], c0[0:H2, 0:CA], ACT.Relu)
                nc.scalar.activation(h2T[:, CA:CA + CB], c1[0:H2, 0:CB], ACT.Relu).then_inc(g2_done, 1)

            def token_scale(g):
                act.wait_ge(var2_done, g + 1)
                nc.scalar.activation(std2[:], mv2[:, :, 1], ACT.Sqrt, bias=epsc[:]).then_inc(std2_done, 1)

            def copy_tokens(g):
                for k, (pa, pb) in enumerate(((c0, c1), (y0, y1))):
                    act.wait_ge(t3_ready, g * 2 + (k + 1))
                    for (lo, hi), ps in zip(SPAN, (pa, pb)):
                        nc.scalar.copy(t_hi[:, k, lo:hi], ps[:, 0:hi - lo]).then_inc(t_hi_done, 1)

            relu_g1(0)
            relu_g2(0)
            token_scale(0)
            copy_tokens(0)

            def group(i, following):
                def gelu(e, halves=range(2)):
                    act.wait_ge(y_ready, i * (NX * J) + max(e, 1) * J)
                    for f in halves:
                        for v, (lo, hi) in enumerate(SPAN_R):
                            n, hi = 4 * e + 2 * f + v, min(hi, J * TP)
                            act.wait_ge(h_ready, i * (4 * NX) + (n + 1))
                            nc.scalar.activation(hT[:, e % 2, f, lo:hi], hbank[n % 3][:, 0:hi - lo], ACT.Gelu,
                                                 bias=b1[:, e, f:f + 1]).then_inc(h_done, 1)

                act.wait_ge(lgT_ready, i + 1)
                for (lo, hi), ps in zip(SPAN_R, (c0, c1)):
                    hi = min(hi, J * TP)
                    last = nc.scalar.copy(lgT[:, lo:hi], ps[0:NX, 0:hi - lo])
                last.then_inc(lgT_done, 1)
                gelu(0, [0])
                act.wait_ge(top_done, i + 1)
                nc.scalar.activation(ex[:], ex[:], ACT.Exp).then_inc(ex_done, 1)
                gelu(0, [1])
                gelu(1)
                act.wait_ge(ct_ready, i + 1)
                nc.scalar.copy(combT[:, 0:CA], c0[0:NX, 0:CA])
                nc.scalar.copy(combT[:, CA:CA + CB], c1[0:NX, 0:CB]).then_inc(ct_done, 1)
                for e in range(2, NX):
                    gelu(e)
                    if following is not None and e == 7:
                        relu_g1(following)
                        relu_g2(following)
                if following is not None:
                    token_scale(following)
                    copy_tokens(following)

            with act.Fori(0, G - 1) as i:
                group(i, i + 1)
            group(G - 1, None)

        @block.vector
        def _(dve):
            step = [0]

            def link(ins):
                step[0] += 1
                ins.then_inc(dve_step, 1)
                dve.wait_ge(dve_step, step[0])

            def moments(t0, t1):
                for t in range(t0, t1):
                    if t % J == 0:
                        dve.wait_ge(x_in[t // J], 16)
                    last = nc.vector.bn_stats(stats[:, t, :], xb[:, t, :])
                link(last)
                for t in range(t0, t1):
                    last = nc.vector.bn_aggr(mv[:, t, :], stats[:, t, :])
                last.then_inc(stats_done, 1)

            def shifts(t0, t1, n):
                dve.wait_ge(std_done, n)
                link(nc.vector.reciprocal(rstd[:, t0:t1], std[:, t0:t1]))
                nc.vector.scalar_tensor_tensor(shift[:, t0:t1], mv[:, t0:t1, 0], -1.0, rstd[:, t0:t1], ALU.mult,
                                               ALU.mult).then_inc(shift_done, 1)

            moments(0, J)
            dve.wait_ge(edges_in, 32)
            shifts(0, J, 1)
            link(nc.vector.tensor_scalar(rnd, src, 1.0 / TP, 0.5 / TP - 0.5, ALU.mult, ALU.add))
            link(nc.vector.tensor_scalar(tile_of, rnd, MAGIC, -MAGIC, ALU.add, ALU.add))
            nc.vector.scalar_tensor_tensor(local, tile_of, -float(TP), src, ALU.mult, ALU.add)
            link(nc.vector.tensor_scalar(rnd, dst, 0.5, -0.25, ALU.mult, ALU.add))
            link(nc.vector.tensor_scalar(val1, rnd, MAGIC, -MAGIC, ALU.add, ALU.add))
            link(nc.vector.scalar_tensor_tensor(odd, val1, -2.0, dst, ALU.mult, ALU.add))
            link(nc.vector.tensor_scalar(odd, odd, float(P), 1.0, ALU.mult, ALU.add))
            nc.vector.tensor_tensor(val2, odd, local, ALU.add)
            moments(J, NT)
            for b in range(NT):
                if b == 4:
                    shifts(J, NT, 2)
                last = nc.vector.tensor_scalar(boh[:, b, :], tile_of, float(b), None, ALU.is_equal)
            link(last)

            link(nc.vector.tensor_tensor_scan(flat_cnt, flat_boh, flat_boh, 0.0, ALU.add, ALU.max))
            end = cnt[:, :, EC - 1]
            nc.vector.tensor_copy(edges_of[:, 0:1], end[:, 0:1])
            nc.vector.tensor_tensor(edges_of[:, 1:NT], end[:, 1:NT], end[:, 0:NT - 1],
                                    ALU.subtract).then_inc(counts_ready, 1)
            dve.wait_ge(totals_ready, 1)
            above, total = agg_ps[0:TP, 0:NT], agg_ps[0:TP, NT:2 * NT]
            link(nc.vector.tensor_reduce(fullest[:], total, AX_X, ALU.max))
            nc.vector.tensor_scalar(spill[:], fullest[:], float(BT * P), None, ALU.is_gt).then_inc(spill_known, 1)
            link(nc.vector.tensor_scalar(adj[:], above, -1.0, None, ALU.add))
            link(nc.vector.tensor_tensor(adj[:, 1:NT], adj[:, 1:NT], end[:, 0:NT - 1], ALU.subtract))
            for lo, hi in ((0, HALF), (HALF, EC)):
                w = hi - lo
                for b in range(NT):
                    last = nc.vector.scalar_tensor_tensor(prod[:, b, 0:w], cnt[:, b, lo:hi], adj[:, b:b + 1],
                                                          boh[:, b, lo:hi], ALU.add, ALU.mult)
                link(last)
                link(nc.vector.tensor_reduce(pos[:, lo:hi], prod[:, :, 0:w].rearrange("p b c -> p c b"),
                                             AX_X, ALU.add))
            link(nc.vector.tensor_scalar(rnd, pos, 1.0 / P, 0.5 / P - 0.5, ALU.mult, ALU.add))
            link(nc.vector.tensor_scalar(rnd, rnd, MAGIC, -MAGIC, ALU.add, ALU.add))
            nc.vector.scalar_tensor_tensor(place_row, rnd, -float(P), pos, ALU.mult, ALU.add)
            nc.vector.scalar_tensor_tensor(place_col, tile_of, float(BT), rnd, ALU.mult, ALU.add)
            link(nc.vector.tensor_scalar(spilled, pos, float(BT * P), None, ALU.is_ge))
            nc.vector.scalar_tensor_tensor(place_col, spilled, NOWHERE, place_col, ALU.mult, ALU.add)
            link(nc.vector.scalar_tensor_tensor(spill_tile, tile_of, 1.0, spilled, ALU.add, ALU.mult))
            link(nc.vector.tensor_scalar(spill_tile, spill_tile, -1.0, None, ALU.add))

            dve.wait_ge(iotas_set, 1)
            dve.wait_ge(pool_set, 1)

            def place(n, b):
                dve.wait_ge(oh_used, n + 1)
                dve.sem_inc(passed, 1)
                nc.vector.tensor_tensor(eqh[:, b, :, :], iota_row[:], columns(place_row, n, P),
                                        ALU.is_equal).then_inc(eqh_ready, 1)
                for u in range(PU):
                    last = nc.vector.tensor_scalar(moh[:, b, u, :], iota_col[:], place_col[:, bass.ds(n * PU + u, 1)],
                                                   None, ALU.is_equal)
                last.then_inc(moh_ready, 1)

            with dve.Fori(0, 5) as i:
                for b in range(OB):
                    place(i * OB + b, b)
            dve.wait_ge(zpart0_done, 1)
            nc.vector.tensor_tensor(zrest, z[:], zparts[:, :, 0, :], ALU.subtract).then_inc(zrest_done, 1)
            with dve.Fori(5, 12) as i:
                for b in range(OB):
                    place(i * OB + b, b)
            dve.wait_ge(gnn_in, 64)
            nc.vector.tensor_scalar(z[:], z[:], wself[:, 0:1], None, ALU.mult)
            dve.wait_ge(zpart1_done, 1)
            nc.vector.tensor_tensor(zparts[:, :, 2, :], zrest, zparts[:, :, 1, :],
                                    ALU.subtract).then_inc(zparts_done, 1)
            with dve.Fori(12, BATCHES // OB) as i:
                for b in range(OB):
                    place(i * OB + b, b)
            place(BATCHES - 1, 0)

            dve.wait_ge(placed, 1)
            got1, got2 = h0[:, 0:ST], h1[:, 0:ST]
            link(nc.vector.tensor_scalar(slot_odd[:], got2, float(P), None, ALU.is_ge))
            nc.vector.scalar_tensor_tensor(slot_dst[:], got1, 2.0, slot_odd[:], ALU.mult, ALU.add)
            nc.vector.scalar_tensor_tensor(slot_src[:], slot_odd[:], -float(P), got2, ALU.mult,
                                           ALU.add).then_inc(slots_done, 1)

            with dve.If(dve.value_load(spill[0:1, 0:1], min_val=0, max_val=1) > 0):
                with dve.Fori(0, EC) as c:
                    dve.wait_ge(spill_landed, c * 16 + 16)
                    dve.sem_inc(passed, 1)
                    nc.vector.tensor_scalar(spill_oh, iota_flat[:, 0:TP], local[:, bass.ds(c, 1)], None, ALU.is_equal)
                    nc.vector.tensor_scalar(spill_in, iota_flat[:, 0:NT], spill_tile[:, bass.ds(c, 1)], None,
                                            ALU.is_equal).then_inc(spill_step, 1)
                    dve.wait_ge(spill_step, c + 1)
                    for part in range(3):
                        last = nc.vector.tensor_tensor(
                            spill_rhs[:, part, :, :],
                            spill_rows[:, part, :].rearrange("p (a h) -> p a h", a=1).to_broadcast([TP, NT, H1]),
                            spill_in.rearrange("p (b a) -> p b a", a=1).to_broadcast([TP, NT, H1]), ALU.mult)
                    last.then_inc(spill_ready, 1)
                dve.wait_ge(spill_total, 1)
                for (b0, b1_), ps in zip(SPILL_BANKS, (m0, m1, y0, y1)):
                    last = nc.vector.tensor_tensor(
                        z[:, b0:b1_, :], z[:, b0:b1_, :],
                        ps[0:TP, 0:(b1_ - b0) * H1].rearrange("p (b h) -> p b h", h=H1), ALU.add)
                last.then_inc(spill_added, 1)
                dve.wait_ge(spill_added, 1)
            dve.sem_inc(values_free, 1)

            def node_onehots(g, j):
                dve.wait_ge(bucket_used, g * J + J + max(j - 1, 0))
                dve.sem_inc(passed, 1)
                sources = slot_src[:, bass.ds(g * (J * BT) + j * BT, BT)]
                nc.vector.tensor_tensor(noh[:, j % 2, :, :], iota_node[:],
                                        sources.rearrange("p (a c) -> p a c", a=1).to_broadcast([P, TP, BT]),
                                        ALU.is_equal).then_inc(noh_ready, 1)

            def drain(g, j):
                dve.wait_ge(bucket_used, g * J + (J + j + 1))
                nc.vector.tensor_reduce(hs[:, j, :], part_sums[j % 2][0:TP, 0:3 * H1].rearrange("p (s h) -> p h s", s=3),
                                        AX_X, ALU.add).then_inc(drained, 1)

            dve.wait_ge(slots_done, 1)
            node_onehots(0, 0)
            node_onehots(0, 1)

            def late_k(t, s):
                dve.wait_ge(ek_done, t + 1)
                dve.wait_ge(ctx_used, t + 1)
                nc.vector.scalar_tensor_tensor(kb2[:, s, :], (y0, y1)[s][0:TP, 0:D], 0.0, ek2[:, s, :],
                                               ALU.max, ALU.add).then_inc(k_done, 1)

            with dve.Fori(NK // 2, NT // 2) as i:
                late_k(i * 2 + 1, 1)
                late_k(i * 2 + 2, 0)

            dve.wait_ge(ctx_ready, 1)
            for c in range(2):
                nc.vector.tensor_tensor(mctx[:, c, :], lg_ps[:, c * P:(c + 1) * P], same_head[:], ALU.mult)
            nc.vector.memset(ksum_of[:], 0.0)
            link(nc.vector.tensor_copy(ksum[:], lg_ps[:, 2 * P:2 * P + 2]))
            for c in range(2):
                heads = slice(c * NH // 2, (c + 1) * NH // 2)
                last = nc.vector.tensor_scalar(ksum_of[:, c, heads],
                                               same_head[:].rearrange("p (h a) -> p h a", a=HD)[:, :, 0],
                                               ksum[:, c:c + 1], None, ALU.mult)
            last.then_inc(ctx_masked, 1)
            dve.wait_ge(w1_hi_done, NX + 1)
            dve.wait_ge(w1_in, 16)
            dve.wait_ge(ffn_in, 48)
            nc.vector.tensor_tensor(rw_lo[:], rw[:], rw_hi[:].bitcast(F32), ALU.subtract)
            for e in range(NX):
                last = nc.vector.tensor_tensor(w1_lo[:, e, :, :], w1[:, e, :, :], w1_hi(e).bitcast(F32), ALU.subtract)
            last.then_inc(w1_lo_done, 1)

            def q_whole(t, s):
                dve.wait_ge(eq_done, t + 1)
                dve.wait_ge(qn_done, t + 1)
                nc.vector.scalar_tensor_tensor(qp[:, s, :], (m0, m1)[s][:, 0:CB], 0.0, eq[:, s, :],
                                               ALU.max, ALU.add).then_inc(qp_done, 1)

            def invert(t, s):
                dve.wait_ge(den_ready, t + 3)
                nc.vector.tensor_scalar(den[:, 0, s, :], (m0, m1)[s][0:TP, 2 * P:2 * P + NH], 1e-6, None,
                                        ALU.max).then_inc(den_read, 1)
                dve.wait_ge(den_read, t + 3)
                nc.vector.reciprocal(den[:, 1, s, :], den[:, 0, s, :]).then_inc(den_inv, 1)

            def divide(t, s):
                dve.wait_ge(den_spread, t + 3)
                dve.wait_ge(mix_ready, t + 1)
                nc.vector.tensor_tensor(qn[:, s, :], (h0, h1)[s][:, 0:CB], qp[:, s, :], ALU.mult
                                        ).then_inc(qn_done, 1)

            def mix_add(t, s):
                dve.wait_ge(mix_ready, t + 3)
                nc.vector.tensor_tensor(tile(xb, t), tile(xb, t), yslot[s], ALU.add).then_inc(mix_added, 1)

            def q_step(t, s):
                invert(t + 1, 1 - s)
                divide(t, s)
                mix_add(t - 1, 1 - s)
                q_whole(t + 2, s)

            dve.sem_inc(qp_done, 2)
            dve.sem_inc(den_read, 2)
            dve.sem_inc(qn_done, 2)
            dve.sem_inc(mix_added, 2)
            dve.wait_ge(bp_added, G)
            for j in range(2):
                drain(0, j)
                node_onehots(0, j + 2)
            q_whole(0, 0)
            q_whole(1, 1)
            invert(0, 0)
            invert(1, 1)
            divide(0, 0)
            q_whole(2, 0)
            for j, pairs in ATTEND_AHEAD:
                with dve.Fori(*pairs) as i:
                    q_step(i * 2 + 1, 1)
                    q_step(i * 2 + 2, 0)
                if j is not None:
                    drain(0, j)
                    if j + 2 < J:
                        node_onehots(0, j + 2)
            invert(NT - 1, 0)
            divide(NT - 2, 1)
            mix_add(NT - 3, 0)
            divide(NT - 1, 0)
            mix_add(NT - 2, 1)
            mix_add(NT - 1, 0)
            drain(0, J - 1)

            link0 = step[0]
            count = [0, 0]

            def chain(ins):
                count[0] += 1
                ins.then_inc(dve_step, 1)
                dve.wait_ge(dve_step, count[1] * CHAIN + (link0 + count[0]))

            def add_self(g):
                dve.wait_ge(drained, g * J + J)
                dve.sem_inc(passed, 1)
                nc.vector.tensor_tensor(hs, hs, z[:, bass.ds(g * J, J), :], ALU.add).then_inc(hs_done, 1)

            def add_graph(g, tiles):
                for j in tiles:
                    dve.wait_ge(g3_ready, g * J + (2, 2, 4, 4, 5)[j])
                    nc.vector.scalar_tensor_tensor(x2[:, j, :], by_token[j], 0.0, tile(xb, g * J + j),
                                                   ALU.max, ALU.add).then_inc(x2_done, 1)
                for j in tiles:
                    dve.wait_ge(x2_done, g * J + (j + 1))
                    last = nc.vector.bn_stats(stats2[:, j, :], x2[:, j, :]).then_inc(stats2_done, 1)

            def variance(g):
                dve.wait_ge(stats2_done, g * J + J)
                dve.sem_inc(passed, 1)
                for j in range(J):
                    last = nc.vector.bn_aggr(mv2[:, j, :], stats2[:, j, :])
                last.then_inc(var2_done, 1)

            def normalize_tokens(g):
                dve.wait_ge(std2_done, g + 1)
                chain(nc.vector.reciprocal(rstd2[:], std2[:]))
                chain(nc.vector.scalar_tensor_tensor(shift2[:], mv2[:, :, 0], -1.0, rstd2[:], ALU.mult, ALU.mult))
                for j in range(J):
                    last = nc.vector.tensor_scalar(tk[:, j, :], x2[:, j, :], rstd2[:, j:j + 1], shift2[:, j:j + 1],
                                                   ALU.mult, ALU.add)
                last.then_inc(tk_done, 1)

            def low_tokens(g):
                for k, (pa, pb) in enumerate(((c0, c1), (y0, y1))):
                    for v, ((lo, hi), ps) in enumerate(zip(SPAN, (pa, pb))):
                        dve.wait_ge(t_hi_done, g * 4 + (k * 2 + v + 1))
                        last = nc.vector.tensor_tensor(t_lo[:, k, lo:hi], ps[:, 0:hi - lo],
                                                       t_hi[:, k, lo:hi].bitcast(F32), ALU.subtract)
                last.then_inc(t_lo_done, 1)

            dve.sem_inc(y_read, 2)
            add_self(0)
            nc.vector.tensor_copy(t_hi[:, :, WR - 1:WR], zeros[:, 0:2].rearrange("p (k a) -> p k a", a=1))
            nc.vector.tensor_copy(t_lo[:, :, WR - 1:WR], zeros[:, 0:2].rearrange("p (k a) -> p k a", a=1)
                                  ).then_inc(pad_set, 1)
            add_graph(0, range(J))
            variance(0)
            normalize_tokens(0)
            low_tokens(0)
            link0, count[0] = link0 + count[0], 0

            def group(i, following):
                count[:] = [0, i]
                dve.wait_ge(y_read, i * (NX * J) + 2)
                dve.wait_ge(stored, i * 16 + 16)
                dve.wait_ge(tk_done, i + 1)
                chain(nc.vector.tensor_tensor(acc, x2, tk, ALU.add))
                dve.wait_ge(lg_ready, i + 1)
                chain(nc.vector.tensor_copy(lg[:].rearrange("p j x -> p (j x)"), c0[0:TP, 0:J * NX]))
                dve.sem_inc(passed, 1)
                for j in range(J):
                    last = nc.vector.max(top[:, j, :], lg[:, j, :])
                chain(last)
                dve.sem_inc(passed, 1)
                for j in range(J):
                    nc.vector.max_index(top_at[:, j, :], top[:, j, :], lg[:, j, :])
                nc.vector.tensor_tensor(ex[:], top[:], top[:, :, 0:1].to_broadcast([TP, J, NX]),
                                        ALU.subtract).then_inc(top_done, 1)
                dve.wait_ge(top_done, i + 1)
                chain(nc.vector.tensor_copy(top_atf[:], top_at[:]))
                dve.wait_ge(ex_done, i + 1)
                chain(nc.vector.tensor_reduce(exs[:], ex[:], AX_X, ALU.add))
                chain(nc.vector.reciprocal(exs[:], exs[:]))
                chain(nc.vector.tensor_tensor(pw[:], ex[:, :, 0:2],
                                              exs[:].rearrange("p (j a) -> p j a", a=1).to_broadcast([TP, J, 2]),
                                              ALU.mult))
                chain(nc.vector.tensor_tensor(pws[:], pw[:, :, 0], pw[:, :, 1], ALU.add))
                chain(nc.vector.tensor_scalar(pws[:], pws[:], 1e-12, None, ALU.max))
                chain(nc.vector.reciprocal(pws[:], pws[:]))
                chain(nc.vector.tensor_tensor(pw[:], pw[:],
                                              pws[:].rearrange("p (j a) -> p j a", a=1).to_broadcast([TP, J, 2]),
                                              ALU.mult))
                for r2 in range(2):
                    last = nc.vector.tensor_tensor(pick[:, r2, :, :], iota_x[:],
                                                   top_atf[:, :, r2:r2 + 1].to_broadcast([TP, J, NX]), ALU.is_equal)
                chain(last)
                for r2 in range(2):
                    last = nc.vector.tensor_tensor(pick[:, r2, :, :], pick[:, r2, :, :],
                                                   pw[:, :, r2:r2 + 1].to_broadcast([TP, J, NX]), ALU.mult)
                chain(last)
                nc.vector.tensor_tensor(comb[:], pick[:, 0, :, :], pick[:, 1, :, :], ALU.add).then_inc(comb_done, 1)
                def add_expert(e, tiles):
                    for j in tiles:
                        q = e * J + j
                        dve.wait_ge(y_ready, i * (NX * J) + (q + J + 1))
                        if e == 1:
                            dve.wait_ge(acc_set, i * J + (j + 1))
                        if e > 1:
                            dve.wait_ge(y_read, i * (NX * J) + (q - J + 3))
                        nc.vector.scalar_tensor_tensor(acc[:, j, :], yslot[q % 2], comb[:, j, e:e + 1], acc[:, j, :],
                                                       ALU.mult, ALU.add).then_inc(y_read, 1)

                dve.wait_ge(comb_done, i + 1)
                add_expert(0, range(J))
                if following is not None:
                    node_onehots(following, 0)
                for j in range(J):
                    dve.wait_ge(b2_ready, i * J + (2, 2, 4, 4, 5)[j])
                    dve.wait_ge(y_read, i * (NX * J) + (j + 3))
                    nc.vector.tensor_tensor(acc[:, j, :], acc[:, j, :], by_token[j], ALU.add).then_inc(acc_set, 1)
                if following is None:
                    for e in range(1, NX):
                        add_expert(e, range(J))
                    return
                for e in range(1, NX - 1):
                    if e <= J:
                        drain(following, e - 1)
                    if e == J:
                        add_self(following)
                    add_expert(e, range(J))
                    if e < J:
                        node_onehots(following, e)
                add_graph(following, range(4))
                add_expert(NX - 1, range(2))
                add_graph(following, [4])
                variance(following)
                add_expert(NX - 1, [2])
                normalize_tokens(following)
                add_expert(NX - 1, [3, 4])
                low_tokens(following)
                assert count[0] == CHAIN, count[0]

            with dve.Fori(0, G - 1) as i:
                group(i, i + 1)
            group(G - 1, None)

        @block.tensor
        def _(pe):
            def zero(ps, start):
                w = ps.shape[-1]
                return nc.tensor.matmul(ps, zeros[:, 0:ps.shape[0]], zeros[:, 0:w], start=start, stop=not start,
                                        skip_group_check=True)

            pe.sem_inc(oh_used, OB)
            pe.sem_inc(kv_ready, 2)
            pe.sem_inc(ctx_used, 2)
            pe.sem_inc(den_ready, 2)
            pe.sem_inc(den_spread, 2)
            pe.sem_inc(mix_ready, 2)
            pe.sem_inc(bucket_used, J)
            pe.sem_inc(spill_summed, 1)
            pe.wait_ge(pool_set, 1)

            nctx = 2 * P + 2
            zero(lg_ps[:, 0:nctx], True)

            def transpose(t, s):
                pe.wait_ge(xn_done, t + 1)
                pe.wait_ge(t1_copied, t + 1)
                for k in range(2):
                    last = nc.tensor.transpose((m0, m1)[s][:, k * TP:(k + 1) * TP],
                                               xn[:, s, k * P:(k + 1) * P], ident[0:TP, 0:TP])
                last.then_inc(t1_ready, 1)

            def z_of(t, s):
                pe.wait_ge(t1_copied, t + 3)
                pe.wait_ge(z_copied, t + 1)
                for k in range(2):
                    last = nc.tensor.matmul((h0, h1)[s][0:TP, 0:H1], xnT[:, s, k, :], w1g[:, k, :],
                                            start=(k == 0), stop=(k == 1))
                last.then_inc(z_ready, 1)

            def k_v(t, s):
                for k in range(2):
                    last = nc.tensor.matmul((y0, y1)[s][0:TP, 0:2 * D], xnT[:, s, k, :], wkv[:, k, :],
                                            start=(k == 0), stop=(k == 1))
                last.then_inc(kv_ready, 1)

            def context(t, s, k_of, v_of):
                pe.wait_ge(k_done, t + 1)
                for c in range(2):
                    f = slice(c * P, (c + 1) * P)
                    nc.tensor.matmul(lg_ps[:, f], v_of[:, s, f], k_of[:, s, f], start=False, stop=False,
                                     skip_group_check=True)
                    last = nc.tensor.matmul(lg_ps[:, 2 * P + c:2 * P + c + 1], k_of[:, s, f], ones[:, 0:1],
                                            start=False, stop=False, skip_group_check=True)
                last.then_inc(ctx_used, 1)

            def step(t, s):
                transpose(t + 1, 1 - s)
                z_of(t, s)
                pe.wait_ge(kv_read, t + 1)
                k_v(t, s)
                context(t - 1, 1 - s, kb, vb)

            transpose(0, 0)
            transpose(1, 1)
            pe.wait_ge(gnn_in, 64)
            pe.wait_ge(kv_in, 16)
            z_of(0, 0)
            k_v(0, 0)
            with pe.Fori(0, 2) as i:
                step(i * 2 + 1, 1)
                step(i * 2 + 2, 0)
            pe.wait_ge(counts_ready, 1)
            nc.tensor.matmul(agg_ps[0:TP, 0:NT], before[:], edges_of[:], start=True, stop=True)
            nc.tensor.matmul(agg_ps[0:TP, NT:2 * NT], ones[:], edges_of[:], start=True, stop=True
                             ).then_inc(totals_ready, 1)
            if NK // 2 > 2:
                with pe.Fori(2, NK // 2) as i:
                    step(i * 2 + 1, 1)
                    step(i * 2 + 2, 0)
            transpose(NK + 1, 0)
            z_of(NK, 1)
            context(NK - 1, 0, kb, vb)
            with pe.Fori(NK // 2 + 1, NT // 2) as i:
                transpose(i * 2 + 1, 1)
                z_of(i * 2, 0)
                transpose(i * 2 + 2, 0)
                z_of(i * 2 + 1, 1)
            z_of(NT - 1, 0)

            got = (h0[:, 0:ST], h1[:, 0:ST])
            pe.wait_ge(z_copied, NT + 2)
            for v in range(2):
                zero(got[v], True)

            def place(n, b):
                pe.wait_ge(moh_ready, n + 1)
                pe.wait_ge(oh_ready, n + 1)
                pe.wait_ge(oh2_ready, n + 1)
                for u in range(PU):
                    nc.tensor.matmul(got[0], soh1[:, b, u, :], moh[:, b, u, :], start=False, stop=False,
                                     skip_group_check=True)
                    last = nc.tensor.matmul(got[1], soh2[:, b, :, u], moh[:, b, u, :], start=False, stop=False,
                                            skip_group_check=True)
                last.then_inc(oh_used, 1)

            with pe.Fori(0, BATCHES // OB) as i:
                for b in range(OB):
                    place(i * OB + b, b)
            place(BATCHES - 1, 0)
            zero(got[0], False)
            zero(got[1], False).then_inc(placed, 1)

            pe.wait_ge(kv_read, NK + 2)
            pe.wait_ge(spill_known, 1)
            with pe.If(pe.value_load(spill[0:1, 0:1], min_val=0, max_val=1) > 0):
                sums = [(ps[0:TP, 0:(b1_ - b0) * H1], b0, b1_)
                        for (b0, b1_), ps in zip(SPILL_BANKS, (m0, m1, y0, y1))]
                for ps, b0, b1_ in sums:
                    zero(ps, True)
                with pe.Fori(0, EC) as c:
                    pe.wait_ge(spill_ready, c + 1)
                    for part in range(3):
                        for ps, b0, b1_ in sums:
                            last = nc.tensor.matmul(ps, spill_oh,
                                                    spill_rhs[:, part, b0:b1_, :].rearrange("p b h -> p (b h)"),
                                                    start=False, stop=False, skip_group_check=True)
                    last.then_inc(spill_summed, 1)
                for ps, b0, b1_ in sums:
                    last = zero(ps, False)
                last.then_inc(spill_total, 1)
                pe.wait_ge(spill_added, 1)

            pe.wait_ge(mix_in, 48)

            def late_k_v(t, s):
                pe.wait_ge(xnT_back, t + (1 - NK))
                pe.wait_ge(k_done, t - 1)
                k_v(t, s)

            late_k_v(NK, 1)
            with pe.Fori(NK // 2, NT // 2 - 1) as i:
                late_k_v(i * 2 + 2, 0)
                context(i * 2 + 1, 1, kb2, vb2)
                late_k_v(i * 2 + 3, 1)
                context(i * 2 + 2, 0, kb2, vb2)
            late_k_v(NT - 1, 0)
            context(NT - 2, 1, kb2, vb2)
            context(NT - 1, 0, kb2, vb2)
            zero(lg_ps[:, 0:nctx], False).then_inc(ctx_ready, 1)

            pe.wait_ge(ctx_masked, 1)
            for c in range(2):
                nc.tensor.matmul((m0, m1)[c][:, 0:D], mctx[:, c, :], wp[:, c, :], start=True, stop=True
                                 ).then_inc(mout_ready, 1)
            pe.wait_ge(mout_done, 2)

            def sum_bucket(g, j):
                if j >= 2:
                    pe.wait_ge(drained, g * J + (j - 1))
                pe.wait_ge(landed[j], g * (16 * BT) + 16 * BT)
                pe.wait_ge(noh_ready, g * J + (j + 1))
                for u in range(BT):
                    last = nc.tensor.matmul(part_sums[j % 2][0:TP, 0:3 * H1], noh[:, j % 2, :, u],
                                            rows[:, j * BT + u, :, :].rearrange("p s h -> p (s h)"),
                                            start=(u == 0), stop=(u == BT - 1))
                last.then_inc(bucket_used, 1)

            sum_bucket(0, 0)
            sum_bucket(0, 1)

            def queries(t, s):
                pe.wait_ge(den_read, t + 1)
                for c in range(2):
                    for k in range(2):
                        last = nc.tensor.matmul((m0, m1)[s][:, c * TP:(c + 1) * TP], wq[:, k, c * P:(c + 1) * P],
                                                xnT_all[:, bass.ds(t * (2 * TP) + k * TP, TP)],
                                                start=(k == 0), stop=(k == 1))
                last.then_inc(q_ready, 1)

            def denominators(t, s):
                pe.wait_ge(qp_done, t + 3)
                for c in range(2):
                    last = nc.tensor.matmul((m0, m1)[s][0:TP, 2 * P:2 * P + NH], qp[:, s, c * TP:(c + 1) * TP],
                                            ksum_of[:, c, :], start=(c == 0), stop=(c == 1))
                last.then_inc(den_ready, 1)

            def spread(t, s):
                pe.wait_ge(widened, t + 1)
                pe.wait_ge(qn_done, t + 1)
                for c in range(2):
                    last = nc.tensor.transpose((h0, h1)[s][:, c * TP:(c + 1) * TP],
                                               wide[:, s, c * P:(c + 1) * P], ident[0:TP, 0:TP])
                last.then_inc(den_spread, 1)

            def attend(t, s):
                pe.wait_ge(qn_done, t + 3)
                pe.wait_ge(mix_added, t + 1)
                for c in range(2):
                    last = nc.tensor.matmul(yslot[s], qn[:, s, c * TP:(c + 1) * TP], mout[:, c, :],
                                            start=(c == 0), stop=(c == 1))
                last.then_inc(mix_ready, 1)

            def q_step(t, s):
                queries(t + 2, s)
                denominators(t + 1, 1 - s)
                spread(t, s)
                attend(t - 1, 1 - s)

            queries(0, 0)
            queries(1, 1)
            denominators(0, 0)
            queries(2, 0)
            denominators(1, 1)
            spread(0, 0)
            for j, pairs in ATTEND_AHEAD:
                with pe.Fori(*pairs) as i:
                    q_step(i * 2 + 1, 1)
                    q_step(i * 2 + 2, 0)
                if j is not None:
                    sum_bucket(0, j)
            denominators(NT - 1, 0)
            spread(NT - 2, 1)
            attend(NT - 3, 0)
            spread(NT - 1, 0)
            attend(NT - 2, 1)
            attend(NT - 1, 0)
            sum_bucket(0, J - 1)

            def graph1(g):
                pe.wait_ge(hs_done, g + 1)
                pe.sem_inc(passed, 1)
                for j in range(J):
                    ps = c0[0:H1, j * TP:(j + 1) * TP] if j < 3 else c1[0:H1, (j - 3) * TP:(j - 2) * TP]
                    last = nc.tensor.transpose(ps, hs[:, j, :], ident[0:TP, 0:TP])
                last.then_inc(g1_ready, 1)

            def graph2(g):
                pe.wait_ge(g1_done, g + 1)
                pe.sem_inc(passed, 1)
                for (lo, hi), ps in zip(SPAN, (c0, c1)):
                    last = nc.tensor.matmul(ps[0:H2, 0:hi - lo], w2g[:], h1T[:, lo:hi], start=True, stop=True)
                last.then_inc(g2_ready, 1)

            def graph3(g, tiles):
                pe.wait_ge(g2_done, g + 1)
                for j in tiles:
                    if j == 4:
                        pe.wait_ge(x2_done, g * J + 2)
                    nc.tensor.matmul(by_token[j], h2T[:, j * TP:(j + 1) * TP], w3g[:],
                                     start=True, stop=True).then_inc(g3_ready, 1)

            def transpose_tokens(g):
                pe.wait_ge(tk_done, g + 1)
                for k, (pa, pb) in enumerate(((c0, c1), (y0, y1))):
                    if k == 1:
                        pe.wait_ge(y_read, g * (NX * J) + 2)
                    for j in range(J):
                        ps = pa[:, j * TP:(j + 1) * TP] if j < 3 else pb[:, (j - 3) * TP:(j - 2) * TP]
                        last = nc.tensor.transpose(ps, tk[:, j, k * P:(k + 1) * P], ident[0:TP, 0:TP])
                    last.then_inc(t3_ready, 1)

            pe.wait_ge(mix_added, NT + 2)
            graph1(0)
            graph2(0)
            graph3(0, range(J))
            transpose_tokens(0)
            pe.wait_ge(w2_in, 16)
            pe.wait_ge(ffn_in, 48)
            pe.wait_ge(w1_lo_done, 1)
            pe.wait_ge(pad_set, 1)
            pe.sem_inc(h_done, 3)
            pe.sem_inc(y_ready, J)

            def group(i, following):
                def product(ps, hi_lo, lo, hi):
                    steps = [(k, w, t) for k in range(2) for w, t in ((0, t_hi), (0, t_lo), (1, t_hi))]
                    for n, (k, w, t) in enumerate(steps):
                        last = nc.tensor.matmul(ps, hi_lo[w][:, k, :], t[:, k, lo:hi],
                                                start=(n == 0), stop=(n == len(steps) - 1))
                    return last

                pe.wait_ge(t_lo_done, i + 1)
                for (lo, hi), ps in zip(SPAN_R, (c0, c1)):
                    last = product(ps[0:NX, 0:hi - lo], (rw_hi[:], rw_lo[:]), lo, hi)
                last.then_inc(lgT_ready, 1)

                def first_layer(e, halves=range(2)):
                    for f in halves:
                        parts = [w[:, :, f * P:(f + 1) * P] for w in (w1_hi(e), w1_lo[:, e, :, :])]
                        for v, (lo, hi) in enumerate(SPAN_R):
                            n = 4 * e + 2 * f + v
                            pe.wait_ge(h_done, i * (4 * NX) + max(n + 1, 3))
                            product(hbank[n % 3][:, 0:hi - lo], parts, lo, hi).then_inc(h_ready, 1)

                def second_layer(e, tiles=range(J)):
                    pe.wait_ge(h_done, i * (4 * NX) + (4 * e + 7))
                    for j in tiles:
                        q = e * J + j
                        pe.wait_ge(y_read, i * (NX * J) + (q + 1))
                        for f in range(2):
                            last = nc.tensor.matmul(yslot[q % 2], hT[:, e % 2, f, j * TP:(j + 1) * TP],
                                                    w2[:, e, f, :], start=(f == 0), stop=(f == 1))
                        last.then_inc(y_ready, 1)

                first_layer(0, [0])
                pe.wait_ge(lgT_done, i + 1)
                pe.sem_inc(passed, 1)
                for j in range(J):
                    last = nc.tensor.transpose(c0[0:TP, j * NX:(j + 1) * NX], lgT[:, j * TP:(j + 1) * TP],
                                               ident[0:NX, 0:NX])
                last.then_inc(lg_ready, 1)
                first_layer(0, [1])
                first_layer(1)
                second_layer(0)
                pe.wait_ge(comb_done, i + 1)
                for j in range(J):
                    ps = c0[0:NX, j * TP:(j + 1) * TP] if j < 3 else c1[0:NX, (j - 3) * TP:(j - 2) * TP]
                    last = nc.tensor.transpose(ps, comb[:, j, :], ident[0:TP, 0:TP])
                last.then_inc(ct_ready, 1)
                first_layer(2)
                pe.wait_ge(ct_done, i + 1)
                for j in range(J):
                    if j == 4:
                        if following is not None:
                            sum_bucket(following, 0)
                        pe.wait_ge(acc_set, i * J + 2)
                    nc.tensor.matmul(by_token[j], combT[:, j * TP:(j + 1) * TP], b2[:],
                                     start=True, stop=True).then_inc(b2_ready, 1)
                for e in range(1, NX):
                    if 2 <= e < NX - 1:
                        first_layer(e + 1)
                    if following is None:
                        second_layer(e)
                        continue
                    if 2 <= e <= J:
                        sum_bucket(following, e - 1)
                    if e == 6:
                        graph1(following)
                    if e == 7:
                        graph3(following, range(4))
                        second_layer(e, range(2))
                        graph3(following, [4])
                        second_layer(e, range(2, J))
                    else:
                        second_layer(e)
                    if e == 6:
                        graph2(following)
                if following is not None:
                    transpose_tokens(following)

            with pe.Fori(0, G - 1) as i:
                group(i, i + 1)
            group(G - 1, None)


CHAIN = 15


def kernel(**inputs):
    import numpy as np
    import concourse.bacc as bacc
    from concourse.bass_utils import run_bass_kernel_spmd

    g = {k: np.asarray(v) for k, v in inputs.items()}
    arrays = {
        "x": g["x"], "src": g["src"], "dst": g["dst"], "w": g["L0_gnn_w"],
        "W1T": g["L0_gnn_W1"].T, "W2T": g["L0_gnn_W2"].T, "W3T": g["L0_gnn_W3"].T,
        "WqT": g["L0_mix_Wq"].T, "WkvT": g["L0_mix_Wkv"].T, "WpT": g["L0_mix_Wproj"].T,
        "bp": g["L0_mix_bproj"], "rT": g["L0_ffn_router_w"].T,
        "w1": g["L0_ffn_w1"], "w2": g["L0_ffn_w2"], "b2": g["L0_ffn_b2"],
        "b1T": g["L0_ffn_b1"].reshape(NX * 2, P).T,
    }
    arrays = {k: np.ascontiguousarray(v) for k, v in arrays.items()}
    nc = bacc.Bacc("TRN2", target_bir_lowering=False, num_devices=1)
    a = {k: nc.dram_tensor(f"in_{k}", v.shape, mybir.dt.from_np(v.dtype), kind="ExternalInput").ap()
         for k, v in arrays.items()}
    out = nc.dram_tensor("out", (N, D), F32, kind="ExternalOutput").ap()
    build(nc, a, out)
    r = run_bass_kernel_spmd(nc, [{f"in_{k}": v for k, v in arrays.items()}], core_ids=[0])
    return r.results[0]["out"]
```
